# Optimizing a Trainium2 kernel written in Bass

```python
import numpy as np
import jax
import jax.numpy as jnp

def _softmax(x, axis=-1):
    return jax.nn.softmax(x, axis=axis)

def _gelu(x):
    return jax.nn.gelu(x, approximate=True)

def _silu(x):
    return jax.nn.silu(x)

def _sigmoid(x):
    return jax.nn.sigmoid(x)

def _layernorm(x, axis=-1, eps=1e-05):
    m = jnp.mean(x, axis=axis, keepdims=True)
    v = jnp.var(x, axis=axis, keepdims=True)
    return (x - m) / jnp.sqrt(v + eps)

def _scatter_add(tgt, idx, src, axis=0):
    return tgt.at[idx].add(src)

def _segment_sum(src, seg, n):
    return jax.ops.segment_sum(src, seg, n)
kernel_name = 'mk_cond_resid_d4_seqx_r8_3bb197'

def setup_inputs(seed: int=0):
    np.random.seed(seed)
    _w = jnp.asarray

    def _rec_inputs():
        import jax
        import jax.numpy as jnp
        _rk = jax.random.key(seed)
        x = -0.000125 + 0.9999 * jax.random.normal(jax.random.fold_in(_rk, 1), (32, 32, 512), jnp.float32)
        _lenS = 32 - jax.random.randint(jax.random.fold_in(_rk, 7), (32,), 0, max(1, 32 // 4) + 1, jnp.int32)
        _lenS2 = 32 - jax.random.randint(jax.random.fold_in(_rk, 8), (32,), 0, max(1, 32 // 4) + 1, jnp.int32)
        itok_B_3_7 = jax.random.randint(jax.random.fold_in(_rk, 11), (32,), 3, 8, jnp.int32)
        itok_B_0_15 = jax.random.randint(jax.random.fold_in(_rk, 12), (32,), 0, 16, jnp.int32)
        itok_B_0_2 = jax.random.randint(jax.random.fold_in(_rk, 13), (32,), 0, 3, jnp.int32)
        itok_Bx16_0_63 = jax.random.randint(jax.random.fold_in(_rk, 14), (32, 16), 0, 64, jnp.int32)
        itok_B_207_1644 = jax.random.randint(jax.random.fold_in(_rk, 15), (32,), 207, 1645, jnp.int32)
        return (x, itok_B_3_7, itok_B_0_15, itok_B_0_2, itok_Bx16_0_63, itok_B_207_1644)
    x, itok_B_3_7, itok_B_0_15, itok_B_0_2, itok_Bx16_0_63, itok_B_207_1644 = _rec_inputs()

    def _L0_cond_setup():
        import jax, jax.numpy as jnp
        import numpy as np
        RANK = 16
        ALPHA = 16.0
        SCALING = ALPHA / RANK
        N_ADAPTERS = 8
        IN_F = 512
        OUT_F = 512
        BATCH = 4
        SEQ = 256
        key = jax.random.key(seed)
        kx, ka, kb, ki = jax.random.split(key, 4)
        x = jax.random.normal(kx, (BATCH, SEQ, IN_F), dtype=jnp.float32)
        A = jax.random.normal(ka, (N_ADAPTERS, OUT_F, RANK), dtype=jnp.float32) * 0.02
        B = jax.random.normal(kb, (N_ADAPTERS, RANK, IN_F), dtype=jnp.float32) * 0.02
        adapter_ids = jax.random.randint(ki, (BATCH,), 0, N_ADAPTERS, dtype=jnp.int32)
        return {'x': x, 'A': A, 'B': B, 'adapter_ids': adapter_ids}
    _L0_cond_all = _L0_cond_setup()
    _L0_cond_in = {k: v for k, v in _L0_cond_all.items() if k in ('A', 'B')}
    del _L0_cond_all

    def _L1_cond_setup():
        import jax, jax.numpy as jnp
        import numpy as np
        MAX_LORAS = 16
        IN, OUT = (512, 512)
        B, S = (8, 256)
        key = jax.random.key(seed)
        k1, k2, k3 = jax.random.split(key, 3)
        x = jax.random.normal(k1, (B, S, IN), dtype=jnp.float32)
        adapter_ids = jax.random.randint(k2, (B,), 0, MAX_LORAS)
        weight = jax.random.normal(k3, (MAX_LORAS, OUT, IN), dtype=jnp.float32) * 0.02
        return {'x': x, 'adapter_ids': adapter_ids, 'weight': weight}
    _L1_cond_all = _L1_cond_setup()
    _L1_cond_in = {k: v for k, v in _L1_cond_all.items() if k in ('weight',)}
    del _L1_cond_all

    def _L2_cond_setup():
        import jax, jax.numpy as jnp
        import numpy as np
        B, S, D_IN, D_OUT = (4, 256, 512, 512)
        R, NUM_LABELERS = (32, 5)
        LORA_SCALING = 16 / 32
        key = jax.random.key(seed)
        k1, k2, k3, k4, k5 = jax.random.split(key, 5)
        x = jax.random.normal(k1, (B, S, D_IN), dtype=jnp.float32)
        labeler_index = jax.random.randint(k2, (B,), 0, NUM_LABELERS, dtype=jnp.int64)
        W = jax.random.normal(k3, (D_OUT, D_IN), dtype=jnp.float32) * 0.02
        lora_A = jax.random.normal(k4, (NUM_LABELERS, D_IN, R), dtype=jnp.float32) * 0.02
        lora_B_w = jax.random.normal(k5, (D_OUT, R), dtype=jnp.float32) * 0.02
        return {'x': x, 'labeler_index': labeler_index, 'W': W, 'lora_A': lora_A, 'lora_B_w': lora_B_w}
    _L2_cond_all = _L2_cond_setup()
    _L2_cond_in = {k: v for k, v in _L2_cond_all.items() if k in ('W', 'lora_A', 'lora_B_w')}
    del _L2_cond_all

    def _L3_cond_setup():
        import jax, jax.numpy as jnp
        import numpy as np
        B, S, HID = (4, 128, 512)
        D, HQ, HK = (128, 32, 8)
        PAGES, PSIZE, NPP = (64, 32, 16)
        THETA = 10000.0
        EPS = 1e-06
        SCALE = 1.0 / float(np.sqrt(D))

        def _rmsnorm(t, w):
            var = jnp.mean(t * t, axis=-1, keepdims=True)
            return t * jax.lax.rsqrt(var + EPS) * w

        def _rope(t, pos):
            inv_freq = 1.0 / THETA ** (jnp.arange(0, D, 2, dtype=jnp.float32) / D)
            freqs = pos[..., None].astype(jnp.float32) * inv_freq
            cos = jnp.cos(freqs)[:, :, None, :]
            sin = jnp.sin(freqs)[:, :, None, :]
            t1, t2 = (t[..., :D // 2], t[..., D // 2:])
            return jnp.concatenate([t1 * cos - t2 * sin, t2 * cos + t1 * sin], axis=-1)
        key = jax.random.key(seed)
        ks = jax.random.split(key, 10)
        x = jax.random.normal(ks[0], (B, S, HID), jnp.float32)
        Wq = jax.random.normal(ks[1], (HQ * D, HID), jnp.float32) * 0.02
        Wk = jax.random.normal(ks[2], (HK * D, HID), jnp.float32) * 0.02
        Wv = jax.random.normal(ks[3], (HK * D, HID), jnp.float32) * 0.02
        Wo = jax.random.normal(ks[4], (HID, HQ * D), jnp.float32) * 0.02
        q_norm_w = jax.random.uniform(ks[5], (D,), jnp.float32)
        k_norm_w = jax.random.uniform(ks[6], (D,), jnp.float32)
        k_cache = jax.random.normal(ks[7], (PAGES, PSIZE, HK, D), jnp.float32)
        v_cache = jax.random.normal(ks[8], (PAGES, PSIZE, HK, D), jnp.float32)
        block_table = jnp.arange(B * NPP, dtype=jnp.int32).reshape(B, NPP)
        cache_seqlens = jax.random.randint(ks[9], (B,), 0, 475).astype(jnp.int32)
        return dict(x=x, Wq=Wq, Wk=Wk, Wv=Wv, Wo=Wo, q_norm_w=q_norm_w, k_norm_w=k_norm_w, k_cache=k_cache, v_cache=v_cache, block_table=block_table, cache_seqlens=cache_seqlens)
    _L3_cond_all = _L3_cond_setup()
    _L3_cond_in = {k: v for k, v in _L3_cond_all.items() if k in ('Wq', 'Wk', 'Wv', 'Wo', 'q_norm_w', 'k_norm_w', 'k_cache', 'v_cache')}
    del _L3_cond_all
    return {'x': x, 'itok_B_3_7': itok_B_3_7, 'itok_B_0_15': itok_B_0_15, 'itok_B_0_2': itok_B_0_2, 'itok_Bx16_0_63': itok_Bx16_0_63, 'itok_B_207_1644': itok_B_207_1644, 'L0_cond_A': _L0_cond_in['A'], 'L0_cond_B': _L0_cond_in['B'], 'L1_cond_weight': _L1_cond_in['weight'], 'L2_cond_W': _L2_cond_in['W'], 'L2_cond_lora_A': _L2_cond_in['lora_A'], 'L2_cond_lora_B_w': _L2_cond_in['lora_B_w'], 'L3_cond_Wq': _L3_cond_in['Wq'], 'L3_cond_Wk': _L3_cond_in['Wk'], 'L3_cond_Wv': _L3_cond_in['Wv'], 'L3_cond_Wo': _L3_cond_in['Wo'], 'L3_cond_q_norm_w': _L3_cond_in['q_norm_w'], 'L3_cond_k_norm_w': _L3_cond_in['k_norm_w'], 'L3_cond_k_cache': _L3_cond_in['k_cache'], 'L3_cond_v_cache': _L3_cond_in['v_cache']}

def reference(x, itok_B_3_7, itok_B_0_15, itok_B_0_2, itok_Bx16_0_63, itok_B_207_1644, L0_cond_A, L0_cond_B, L1_cond_weight, L2_cond_W, L2_cond_lora_A, L2_cond_lora_B_w, L3_cond_Wq, L3_cond_Wk, L3_cond_Wv, L3_cond_Wo, L3_cond_q_norm_w, L3_cond_k_norm_w, L3_cond_k_cache, L3_cond_v_cache):
    import jax
    import jax.numpy as jnp

    def _L0_cond_ref(x, A, B, adapter_ids):
        import jax, jax.numpy as jnp
        import numpy as np
        RANK = 16
        ALPHA = 16.0
        SCALING = ALPHA / RANK
        N_ADAPTERS = 8
        IN_F = 512
        OUT_F = 512
        BATCH = 4
        SEQ = 256
        B_sel = B[adapter_ids]
        A_sel = A[adapter_ids]
        Bx = jnp.einsum('bni,bri->bnr', x, B_sel)
        out = jnp.einsum('bnr,bor->bno', Bx, A_sel)
        return out * SCALING

    def _L1_cond_ref(x, adapter_ids, weight):
        import jax, jax.numpy as jnp
        import numpy as np
        MAX_LORAS = 16
        IN, OUT = (512, 512)
        B, S = (8, 256)
        w = weight[adapter_ids]
        return jnp.einsum('bsi,boi->bso', x, w)

    def _L2_cond_ref(x, labeler_index, W, lora_A, lora_B_w):
        import jax, jax.numpy as jnp
        import numpy as np
        B, S, D_IN, D_OUT = (4, 256, 512, 512)
        R, NUM_LABELERS = (32, 5)
        LORA_SCALING = 16 / 32
        base = jnp.einsum('bsi,oi->bso', x, W)
        labelers_A = lora_A[labeler_index]
        low = jnp.einsum('bsi,bir->bsr', x, labelers_A)
        delta = jnp.einsum('bsr,or->bso', low, lora_B_w) * LORA_SCALING
        return base + delta

    def _L3_cond_ref(x, Wq, Wk, Wv, Wo, q_norm_w, k_norm_w, k_cache, v_cache, block_table, cache_seqlens):
        import jax, jax.numpy as jnp
        import numpy as np
        B, S, HID = (4, 128, 512)
        D, HQ, HK = (128, 32, 8)
        PAGES, PSIZE, NPP = (64, 32, 16)
        THETA = 10000.0
        EPS = 1e-06
        SCALE = 1.0 / float(np.sqrt(D))

        def _rmsnorm(t, w):
            var = jnp.mean(t * t, axis=-1, keepdims=True)
            return t * jax.lax.rsqrt(var + EPS) * w

        def _rope(t, pos):
            inv_freq = 1.0 / THETA ** (jnp.arange(0, D, 2, dtype=jnp.float32) / D)
            freqs = pos[..., None].astype(jnp.float32) * inv_freq
            cos = jnp.cos(freqs)[:, :, None, :]
            sin = jnp.sin(freqs)[:, :, None, :]
            t1, t2 = (t[..., :D // 2], t[..., D // 2:])
            return jnp.concatenate([t1 * cos - t2 * sin, t2 * cos + t1 * sin], axis=-1)
        bsz, seqlen, _ = x.shape
        q = jnp.einsum('bsd,ed->bse', x, Wq).reshape(bsz, seqlen, HQ, D)
        k = jnp.einsum('bsd,ed->bse', x, Wk).reshape(bsz, seqlen, HK, D)
        v = jnp.einsum('bsd,ed->bse', x, Wv).reshape(bsz, seqlen, HK, D)
        q = _rmsnorm(q, q_norm_w)
        k = _rmsnorm(k, k_norm_w)
        pos = cache_seqlens[:, None] + jnp.arange(seqlen)[None, :]
        q = _rope(q, pos)
        k = _rope(k, pos)
        L = NPP * PSIZE
        kc = k_cache[block_table].reshape(bsz, L, HK, D)
        vc = v_cache[block_table].reshape(bsz, L, HK, D)
        k_all = jnp.concatenate([kc, k], axis=1)
        v_all = jnp.concatenate([vc, v], axis=1)
        valid_c = jnp.arange(L)[None, :] < cache_seqlens[:, None]
        valid = jnp.concatenate([valid_c, jnp.ones((bsz, seqlen), dtype=bool)], axis=1)
        rep = HQ // HK
        k_all = jnp.repeat(k_all, rep, axis=2)
        v_all = jnp.repeat(v_all, rep, axis=2)
        scores = jnp.einsum('bqhd,bkhd->bhqk', q, k_all) * SCALE
        scores = jnp.where(valid[:, None, None, :], scores, -1e+30)
        probs = jax.nn.softmax(scores, axis=-1)
        o = jnp.einsum('bhqk,bkhd->bqhd', probs, v_all)
        o = o.reshape(bsz, seqlen, HQ * D)
        return jnp.einsum('bse,de->bsd', o, Wo)
    x = x + _L0_cond_ref(x, L0_cond_A, L0_cond_B, itok_B_3_7)
    x = x + _L1_cond_ref(x, itok_B_0_15, L1_cond_weight)
    x = x + _L2_cond_ref(x, itok_B_0_2, L2_cond_W, L2_cond_lora_A, L2_cond_lora_B_w)
    x = x + _L3_cond_ref(x, L3_cond_Wq, L3_cond_Wk, L3_cond_Wv, L3_cond_Wo, L3_cond_q_norm_w, L3_cond_k_norm_w, L3_cond_k_cache, L3_cond_v_cache, itok_Bx16_0_63, itok_B_207_1644)
    return x

_drawn_inputs = setup_inputs


def setup_inputs(seed=0):
    import zlib

    import numpy as np

    out = dict(_drawn_inputs(seed))
    spreads = {}
    factors = {'L3_cond_Wk': 39.463,
     'L3_cond_Wv': 57.206,
     'L3_cond_q_norm_w': 2.968,
     'L3_cond_k_norm_w': 41.997,
     'L3_cond_k_cache': 8.0,
     'L3_cond_v_cache': 8.0}
    for name, (base, spread) in spreads.items():
        noise = np.random.default_rng([zlib.crc32(name.encode()), seed]).standard_normal(out[name].shape)
        drawn = base * np.exp(spread * noise) if base else spread * noise
        out[name] = jnp.asarray(drawn.astype(out[name].dtype))
    for name, factor in factors.items():
        out[name] = (out[name] * factor).astype(out[name].dtype)
    return out
```

```python
from contextlib import ExitStack

import concourse.bass as bass
from concourse import mybir

F32 = mybir.dt.float32
F32R = mybir.dt.float32r
BF16 = mybir.dt.bfloat16
F16 = mybir.dt.float16
I32 = mybir.dt.int32
I16 = mybir.dt.int16
ALU = mybir.AluOpType
ACT = mybir.ActivationFunctionType
ds = bass.ds

P = 128
B, S, DM = 32, 32, 512
T = B * S
KC = DM // P
TC = T // 512
TT = T // P
BPT = P // S
BPC = 512 // S
HD = 128
HQ, HK = 32, 8
REP = HQ // HK
HALVES = 2
KVH = HK // HALVES
QH = HQ // HALVES
PAGES, PSIZE, NPP = 64, 32, 16
L = NPP * PSIZE
KEYS = L + S
KPAD = 640
KCH = KPAD // P
VCH = L // P
SLOTS = KVH + QH
BLK = 6
OBLK = 4
NBLK = BLK + OBLK
BW = KC * 512
QKT = 5 * TT
UNITS = B * KVH
SPP = 12
PPP = NPP - SPP
PTA = 3
R0, N0 = 16, 8
R2, N2 = 32, 5
EPS = 1e-6
SCALE = HD ** -0.5
NEG = -1e30
BIG = 3e38
TWO_PI = 6.283185307179586
ROUND = 1.5 * 2.0 ** 23
PI_A = 6.28125
PI_B = 0.0019350051879882812
PI_C = TWO_PI - PI_A - PI_B
PI_IN = 3.1415925
C_ID, C_P16, C_P32, C_M32, C_P, C_FREQ = 0, 128, 129, 130, 131, 132
C_N = C_FREQ + HD // 2


def build(nc, a, out):
    with ExitStack() as ctx:
        def sb(name, shape, dt=F32):
            return ctx.enter_context(nc.sbuf_tensor(name, shape, dt))

        def sem(name):
            return ctx.enter_context(nc.semaphore(name))

        x_t = sb("x_t", [P, KC, T])
        x_hi = sb("x_hi", [P, KC, T], F32R)
        x_lo = sb("x_lo", [P, KC, T], F32R)
        rope_c = sb("rope_c", [P, 2, TT, HD])
        rope_s = sb("rope_s", [P, 2, TT, HD])
        consts = sb("consts_sb", [P, C_N])
        ident = consts[:, C_ID:C_ID + P]
        iota16 = sb("iota16", [P, L], F16)
        len_b = sb("len_b", [P, B + 1])
        v_rows = sb("v_rows", [P, HALVES, B, VCH], I16)
        k_rows = sb("k_rows", [P, HALVES, B, PPP], I16)
        v_idx = sb("v_idx", [P, 2, VCH], I32)
        k_idx = sb("k_idx", [P, 2, PPP], I32)
        ids_row = sb("ids_row", [1, B], I32)
        pages_row = sb("pages_row", [1, B, NPP], I32)
        stat = sb("stat", [P, 2, 6, 4])
        SQ, VAR, INV, Y0, NT, RSTD = range(6)
        sm_min = sb("sm_min", [P, 2])
        row_sum = sb("row_sum", [P, 2])
        row_inv = sb("row_inv", [P, 2])
        at = [-(-nc.sbuf_base // 32) * 32]

        def place(name, shape, dt=F32, p=P):
            t = nc.alloc_sbuf_tensor_at(name, [p] + shape, dt, offset=at[0])
            size = mybir.dt.size(dt)
            for n in shape:
                size *= n
            at[0] += -(-size // 32) * 32
            return t

        store_at = at[0]
        qk = place("qk", [B, SLOTS, S])
        region = at[0]
        at[0] = store_at
        ids0 = place("ids0", [B], I32)
        ids2 = place("ids2", [B], I32)
        mask0 = place("mask0", [B])
        mask2 = place("mask2", [B])
        mask24 = place("mask24", [B])
        lens = place("lens", [B], I32)
        len_tok = place("len_tok", [TT], I32)
        pos = place("pos", [TT])
        bt_v = place("bt_v", [B, VCH], I32)
        bt_k = place("bt_k", [B, PPP], I32)
        norm_w = place("norm_w", [2, HD])
        iota_f = place("iota_f", [L])
        ang = place("ang", [TT, HD // 2])
        cyc = place("cyc", [TT, HD // 2])
        turns = place("turns", [TT, HD // 2])
        sin_t = place("sin_t", [TT, HD // 2])
        sin_h = place("sin_h", [TT, HD // 2])
        cos_t = place("cos_t", [TT, HD // 2])
        at[0] = region
        w_exp = place("w_exp", [4, KC, DM])
        w0b = place("w0b", [KC, P])
        w0a = place("w0a", [DM])
        w2 = place("w2", [KC, DM])
        w2a = place("w2a", [KC, N2 * R2])
        w2b = place("w2b", [DM])
        low = place("low", [T])
        low4 = place("low4", [T], p=R2)
        at[0] = region
        w_in = place("w_in", [BW])
        w_hi = place("w_hi", [BW], F32R), place("w_hi1", [BW], F32R)
        w_lo = place("w_lo", [BW], F32R), place("w_lo1", [BW], F32R)
        work = at[0]
        r_cos = place("r_cos", [2, 512])
        r_sin = place("r_sin", [2, 512])
        r_out = place("r_out", [2, 512])
        b_sq = place("b_sq", [512])
        at[0] = work
        o_hi = place("o_hi", [2, 2, 512], F32R)
        o_lo = place("o_lo", [2, 2, 512], F32R)
        at[0] = region
        k_buf = place("k_buf", [2, NPP, KVH, S])
        v_buf = place("v_buf", [2, KCH, KVH * HD])
        qk_st = place("qk_st", [2, SLOTS, S])
        sm = place("sm", [2, KEYS])
        pr = place("pr", [2, KPAD])
        pt = place("pt", [2, KPAD])
        o_sb = place("o_sb", [2, P])
        mask = place("mask", [2, KEYS], BF16)

        ps = ctx.enter_context(nc.psum_tensor("ps", [P, 8, 512], F32))

        ids_in, const_in, setup_in = sem("ids_in"), sem("const_in"), sem("setup_in")
        x_in = [sem(f"x_in{c}") for c in range(TC)]
        w0_in, w2_in = sem("w0_in"), sem("w2_in")
        exp_in = [sem(f"exp_in{s}") for s in range(4)]
        w_in_done = sem("w_in_done")
        q_in = [sem(f"q_in{p}") for p in range(2)]
        k_in = [sem(f"k_in{p}") for p in range(2)]
        k_in2 = [sem(f"k_in2{p}") for p in range(2)]
        v_in = [sem(f"v_in{p}") for p in range(2)]
        vn_in = [sem(f"vn_in{p}") for p in range(2)]
        v_stored = [sem(f"v_stored{p}") for p in range(2)]
        out_stored = sem("out_stored")
        settled = sem("settled")
        setup = sem("setup")
        masks_ready = sem("masks_ready")
        rad_ready, sin_ready = sem("rad_ready"), sem("sin_ready")
        l0_low_done, l0_low_masked, l0_done, l0_added = (
            sem("l0_low_done"), sem("l0_low_masked"), sem("l0_done"), sem("l0_added"))
        l1_done, l1_added = sem("l1_done"), sem("l1_added")
        l2_low_done, l2_low_masked, l2_done, l2_added = (
            sem("l2_low_done"), sem("l2_low_masked"), sem("l2_done"), sem("l2_added"))
        x_hi_ready, x_lo_ready = sem("x_hi_ready"), sem("x_lo_ready")
        w_hi_done, w_lo_done = sem("w_hi_done"), sem("w_lo_done")
        proj_done, sq_done, var_done, inv_done, y0_done = (
            sem("proj_done"), sem("sq_done"), sem("var_done"), sem("inv_done"), sem("y0_done"))
        newton, rstd_done, roped, summed, rn_done = (
            sem("newton"), sem("rstd_done"), sem("roped"), sem("summed"), sem("rn_done"))
        qk_turned, qk_stored, v_copied = sem("qk_turned"), sem("qk_stored"), sem("v_copied")
        v_padded, idx_copied, mask_done = sem("v_padded"), sem("idx_copied"), sem("mask_done")
        s_done, max_done, exp_done, p_turned = (
            sem("s_done"), sem("max_done"), sem("exp_done"), sem("p_turned"))
        pt_a, pt_b, pv_done, inv_l, o_norm, o_turned, o_stored = (
            sem("pt_a"), sem("pt_b"), sem("pv_done"), sem("inv_l"), sem("o_norm"),
            sem("o_turned"), sem("o_stored"))
        o_hi_ready, o_lo_ready, d_done, d_added = (
            sem("o_hi_ready"), sem("o_lo_ready"), sem("d_done"), sem("d_added"))
        D_AHEAD, ADD_AHEAD, LO_AHEAD = 8, 8, 4

        block = ctx.enter_context(nc.Block())

        def chunk(c):
            return slice(512 * c, 512 * (c + 1))

        def tile(t):
            return slice(P * t, P * (t + 1))

        def b_done(eng, g):
            for p in range(2):
                eng.wait_ge(v_stored[p], 64 * g + 64)

        def settle(eng):
            eng.sem_inc(settled, 1)

        @block.sync
        def _(sp):
            sp.dma_start(ids_row[:], a["ids1"].unsqueeze(0)).then_inc(ids_in, 16)
            sp.dma_start(x_t[:, :, chunk(0)], a["x_t"][:, :, chunk(0)]).then_inc(x_in[0], 16)
            sp.dma_start(w0b[:], a["l0_b"]).then_inc(w0_in, 16)
            sp.dma_start(w0a[:], a["l0_a"]).then_inc(w0_in, 16)
            sp.dma_start(x_t[:, :, chunk(1)], a["x_t"][:, :, chunk(1)]).then_inc(x_in[1], 16)
            sp.wait_ge(ids_in, 16)

            def load_expert(b, s):
                e = sp.value_load(ids_row[0:1, ds(b, 1)], min_val=0, max_val=15)
                if not isinstance(b, int):
                    sp.wait_ge(l1_done, b - 3)
                sp.dma_start(w_exp[:, s], a["l1_w"][ds(e, 1)].rearrange("e p k n -> p (e k) n")
                             ).then_inc(exp_in[s], 16)

            for s in range(4):
                load_expert(s, s)
            sp.dma_start(w2[:], a["l2_w"]).then_inc(w2_in, 16)
            sp.dma_start(w2a[:], a["l2_a"]).then_inc(w2_in, 16)
            for r in range(P // R2):
                sp.dma_start(w2b[R2 * r:R2 * (r + 1)], a["l2_b"]).then_inc(w2_in, 16)
            with sp.Fori(1, B // 4) as i:
                for s in range(4):
                    load_expert(4 * i + s, s)
            sp.wait_ge(l1_done, B)

            def load_block(n):
                sp.wait_ge(w_lo_done, 4 * n + LO_AHEAD)
                sp.dma_start(w_in[:], a["l3_w"][ds(n, 1)].rearrange("n p w -> p (n w)")
                             ).then_inc(w_in_done, 16)

            def load_batch(g, b, p, first):
                settle(sp)
                pages = nc.values_load_multi_w_load_instructions(
                    pages_row[0:1, ds(b, 1), 0:SPP], engines=[mybir.EngineType.SP], min_val=0,
                    max_val=PAGES - 1, skip_runtime_bounds_check_because="ids of cache pages")[1]
                if not first:
                    sp.wait_ge(s_done, UNITS * g + 4 * b - 4)
                sp.dma_start(qk_st[:, p], qk[:, ds(b, 1)].rearrange("p b h t -> p (b h) t")
                             ).then_inc(q_in[p], 16)
                for j in range(SPP):
                    sp.dma_start(
                        k_buf[:, p, j],
                        a["k_t"][ds(PAGES * g + pages[j], 1)].rearrange("n p h t -> p (n h) t")
                    ).then_inc(k_in[p], 16)
                if first:
                    sp.wait_ge(v_padded, 2 * g + 2)
                else:
                    sp.wait_ge(pv_done, UNITS * g + 4 * b - 4)
                sp.dma_start(v_buf[0:S, p, VCH], a["v_new"][ds(B * g + b, 1)].rearrange("n t w -> (n t) w")
                             ).then_inc(vn_in[p], 16)

            with sp.Fori(0, HALVES) as g:
                with sp.Fori(0, BLK) as j:
                    load_block(NBLK * g + j)
                for t in range(TT):
                    sp.wait_ge(v_copied, 8 * g + (t + 1))
                    sp.dma_start(
                        a["v_new"][ds(B * g + BPT * t, BPT)].rearrange("n t w -> (n t) w"),
                        r_sin[:, t % 2]).then_inc(v_stored[t % 2], 16)
                b_done(sp, g)
                for b in range(2):
                    load_batch(g, b, b, True)
                with sp.Fori(1, B // 2) as i:
                    for p in range(2):
                        load_batch(g, 2 * i + p, p, False)
                sp.wait_ge(o_stored, B * g + B)
                settle(sp)
                with sp.Fori(BLK, NBLK) as j:
                    load_block(NBLK * g + j)
            for c in range(TC):
                for oc in range(KC):
                    sp.wait_ge(d_added, ADD_AHEAD + 8 * (HALVES - 1) + KC * c + oc + 1)
                    sp.dma_start(out[:, oc, chunk(c)], x_t[:, oc, chunk(c)]).then_inc(out_stored, 16)
            sp.wait_ge(out_stored, 16 * TC * KC)

        @block.gpsimd
        def _(pool):
            def split_low(g, j, part):
                n, par = j
                cols = chunk(part)
                pool.wait_ge(w_hi_done, 4 * n + (part + 1))
                nc.gpsimd.tensor_tensor(w_lo[par][:, cols], w_in[:, cols],
                                        w_hi[par][:, cols].bitcast(F32),
                                        ALU.subtract).then_inc(w_lo_done, 1)

            def qk_tile(g, j, t, first, par):
                m = 8 * j + t
                pool.wait_ge(roped, QKT * g + m + 1)
                c4 = r_cos[:, t % 2].rearrange("p (h d) -> p h d", h=4)
                s4 = r_sin[:, t % 2].rearrange("p (h d) -> p h d", h=4)
                half = HD // 2
                nc.gpsimd.tensor_tensor(c4[:, :, 0:half], c4[:, :, 0:half], s4[:, :, half:HD], ALU.add)
                nc.gpsimd.tensor_tensor(c4[:, :, half:HD], c4[:, :, half:HD], s4[:, :, 0:half],
                                        ALU.add).then_inc(summed, 1)
                pool.wait_ge(y0_done, QKT * g + m + 1)
                y, v = stat[:, t % 2, Y0], stat[:, t % 2, VAR]
                w, r = stat[:, t % 2, NT], stat[:, t % 2, RSTD]
                nc.gpsimd.tensor_tensor(w, y, y, ALU.mult).then_inc(newton, 1)
                pool.wait_ge(newton, 3 * (QKT * g + m) + 1)
                nc.gpsimd.tensor_tensor(w, w, v, ALU.mult).then_inc(newton, 1)
                pool.wait_ge(newton, 3 * (QKT * g + m) + 2)
                settle(pool)
                nc.gpsimd.tensor_scalar(w, w, -0.5, 1.5, ALU.mult, ALU.add).then_inc(newton, 1)
                pool.wait_ge(newton, 3 * (QKT * g + m) + 3)
                if not (first and t < 2):
                    pool.wait_ge(rn_done, QKT * g + m - 1)
                nc.gpsimd.tensor_tensor(r, y, w, ALU.mult).then_inc(rstd_done, 1)
                if 3 <= t < 7:
                    split_low(g, (NBLK * g + j + 1, 1 - par), t - 3)

            def fetch(g, b, p, first):
                if not first:
                    pool.wait_ge(s_done, UNITS * g + 4 * b - 4)
                n = B * g + b
                row = k_rows[:, :].rearrange("p g b c -> p (g b) c")
                nc.gpsimd.tensor_copy(k_idx[:, p], row[:, ds(n, 1)]).then_inc(idx_copied, 1)
                pool.wait_ge(idx_copied, 2 * n + 1)
                settle(pool)
                for j in range(PPP):
                    pool.indirect_dma_start(
                        k_buf[:, p, SPP + j].rearrange("p h t -> p (h t)"), None, a["k_rows"],
                        bass.IndirectOffsetOnAxis(k_idx[:, p, j:j + 1], 0)).then_inc(k_in2[p], 16)
                if not first:
                    pool.wait_ge(pv_done, UNITS * g + 4 * b - 4)
                row = v_rows[:, :].rearrange("p g b c -> p (g b) c")
                nc.gpsimd.tensor_copy(v_idx[:, p], row[:, ds(n, 1)]).then_inc(idx_copied, 1)
                pool.wait_ge(idx_copied, 2 * n + 2)
                settle(pool)
                for c in range(VCH):
                    pool.indirect_dma_start(
                        v_buf[:, p, c], None, a["v_rows"],
                        bass.IndirectOffsetOnAxis(v_idx[:, p, c:c + 1], 0)).then_inc(v_in[p], 16)

            with pool.Fori(0, HALVES) as g:
                for part in range(4):
                    split_low(g, (NBLK * g, 0), part)
                for t in range(TT):
                    qk_tile(g, 0, t, True, 0)
                with pool.Fori(0, 2) as i:
                    for e in range(2):
                        for t in range(TT):
                            qk_tile(g, 2 * i + (1 + e), t, False, 1 - e)
                b_done(pool, g)
                settle(pool)
                for p in range(2):
                    nc.gpsimd.memset(v_buf[:, p, VCH], 0.0).then_inc(v_padded, 1)
                for b in range(2):
                    fetch(g, b, b, True)
                with pool.Fori(1, B // 2) as i:
                    for p in range(2):
                        fetch(g, 2 * i + p, p, False)
                with pool.Fori(0, 2) as i:
                    for e in range(2):
                        for part in range(4):
                            split_low(g, (NBLK * g + BLK + 2 * i + e, e), part)

        @block.scalar
        def _(act):
            act.dma_start(consts[:], a["consts"]).then_inc(const_in, 16)
            act.dma_start(ids0[:], a["ids0"].partition_broadcast(P)).then_inc(const_in, 16)
            act.dma_start(ids2[:], a["ids2"].partition_broadcast(P)).then_inc(const_in, 16)
            act.dma_start(lens[:], a["lens"].partition_broadcast(P)).then_inc(setup_in, 16)
            for q in range(4):
                rows = slice(32 * q, 32 * (q + 1))
                act.dma_start(len_tok[rows], a["lens_q"][q].partition_broadcast(S)).then_inc(setup_in, 16)
                act.dma_start(bt_v[rows], a["pages_q"][q].partition_broadcast(PSIZE)).then_inc(setup_in, 16)
            act.dma_start(bt_k[:], a["pages_k"].partition_broadcast(P)).then_inc(setup_in, 16)
            act.dma_start(norm_w[:, 0], a["k_norm"].partition_broadcast(P)).then_inc(setup_in, 16)
            act.dma_start(norm_w[:, 1], a["q_norm"].partition_broadcast(P)).then_inc(setup_in, 16)
            act.dma_start(iota_f[:], a["iota"].partition_broadcast(P)).then_inc(setup_in, 16)
            act.dma_start(pages_row[:], a["pages"].unsqueeze(0)).then_inc(setup_in, 16)
            act.wait_ge(rad_ready, 1)
            nc.scalar.activation(sin_t[:], ang[:], ACT.Sin)
            nc.scalar.activation(sin_h[:], ang[:], ACT.Sin, scale=0.5).then_inc(sin_ready, 1)
            for c in range(TC):
                for kc in range(KC):
                    act.wait_ge(l2_added, KC * c + kc + 1)
                    nc.scalar.copy(x_hi[:, kc, chunk(c)], x_t[:, kc, chunk(c)]).then_inc(x_hi_ready, 1)

            def split_high(n, par, part):
                cols = chunk(part)
                if part == 0:
                    act.wait_ge(w_in_done, 16 * n + 16)
                nc.scalar.copy(w_hi[par][:, cols], w_in[:, cols]).then_inc(w_hi_done, 1)

            def store_qk(g, m, j, t):
                act.wait_ge(qk_turned, QKT * g + m + 1)
                nc.scalar.copy(
                    qk[:, BPT * t:BPT * (t + 1), ds(4 * j, 4), :],
                    ps[:, 4 + t % 2].rearrange("p (h b s) -> p b h s", h=4, b=BPT)
                ).then_inc(qk_stored, 1)

            def qk_tile(g, j, t, first, par):
                m = 8 * j + t
                act.wait_ge(proj_done, 48 * g + m + 1)
                if not (first and t == 0):
                    act.wait_ge(sq_done, QKT * g + m)
                for h in range(4):
                    ins = nc.scalar.activation(b_sq[:, tile(h)], ps[:, t % 4, tile(h)], ACT.Square,
                                               accum_out=stat[:, t % 2, SQ, h:h + 1])
                ins.then_inc(sq_done, 1)
                act.wait_ge(inv_done, QKT * g + m + 1)
                if not (first and t < 2):
                    act.wait_ge(rstd_done, QKT * g + m - 1)
                nc.scalar.activation(stat[:, t % 2, Y0], stat[:, t % 2, INV], ACT.Sqrt).then_inc(y0_done, 1)
                if t >= 2:
                    store_qk(g, m - 2, j, t - 2)
                elif not first:
                    store_qk(g, m - 2, j - 1, t + 6)
                if 3 <= t < 7:
                    split_high(NBLK * g + j + 1, 1 - par, t - 3)

            def exp_unit(g, s, c):
                act.wait_ge(max_done, UNITS * g + s + 1)
                if c >= 2:
                    act.wait_ge(p_turned, UNITS * g + s - 1)
                nc.scalar.activation(pr[:, c % 2, 0:KEYS], sm[:, c % 2], ACT.Exp,
                                     bias=sm_min[:, c % 2:c % 2 + 1], scale=-1.0,
                                     accum_out=row_sum[:, c % 2:c % 2 + 1]).then_inc(exp_done, 1)

            def copy_pt(g, s, c):
                act.wait_ge(p_turned, UNITS * g + s + 1)
                if c >= 2:
                    act.wait_ge(pv_done, UNITS * g + s - 1)
                nc.scalar.copy(pt[:, c % 2, PTA * P:KPAD], ps[:, 5, 0:KPAD - PTA * P]).then_inc(pt_b, 1)

            def store_o(g, b, s):
                act.wait_ge(o_turned, UNITS * g + s + 1)
                nc.scalar.copy(qk[:, ds(b, 1), KVH:SLOTS, :].rearrange("p b h t -> p (b h t)"),
                               ps[:, 7, :]).then_inc(o_stored, 1)

            def unit_step(g, i, e, c):
                s = 8 * i + e
                if c < UNITS:
                    exp_unit(g, s, c)
                if c >= 4 and c % 4 == 2 and c >= 6:
                    store_o(g, 2 * i + (e // 4 - 1), s - 3)
                if 1 <= c <= UNITS:
                    copy_pt(g, s - 1, c - 1)

            with act.Fori(0, HALVES) as g:
                act.wait_ge(d_done, 16 * g + 4)
                for part in range(4):
                    split_high(NBLK * g, 0, part)
                for t in range(TT):
                    qk_tile(g, 0, t, True, 0)
                with act.Fori(0, 2) as i:
                    for e in range(2):
                        for t in range(TT):
                            qk_tile(g, 2 * i + (1 + e), t, False, 1 - e)
                for t in range(TT):
                    if t < 2:
                        store_qk(g, QKT - 2 + t, 4, 6 + t)
                        act.wait_ge(summed, QKT * g + QKT - 1 + t)
                    else:
                        act.wait_ge(v_stored[t % 2], 64 * g + 16 * (t // 2))
                    act.wait_ge(proj_done, 48 * g + QKT + t + 1)
                    nc.scalar.copy(r_sin[:, t % 2], ps[:, t % 4]).then_inc(v_copied, 1)
                b_done(act, g)
                for c in range(8):
                    unit_step(g, 0, c, c)
                with act.Fori(1, UNITS // 8) as i:
                    for e in range(8):
                        unit_step(g, i, e, 8 + e)
                for e in range(3):
                    unit_step(g, UNITS // 8, e, UNITS + e)
                act.wait_ge(o_stored, B * g + B)
                with act.Fori(0, 2) as i:
                    for e in range(2):
                        act.wait_ge(d_done, 16 * g + 8 * i + 4 * e + D_AHEAD - 4)
                        for part in range(4):
                            split_high(NBLK * g + BLK + 2 * i + e, e, part)
                        for c in range(TC):
                            for pair in range(2):
                                k = 4 * e + 2 * c + pair
                                act.wait_ge(d_done, 16 * g + 8 * i + k + D_AHEAD - 1)
                                nc.scalar.copy(
                                    o_hi[:, pair].rearrange("p h (b t) -> p b h t", t=S),
                                    qk[:, 16 * c:16 * (c + 1), ds(8 * i + (KVH + 4 * e + 2 * pair), 2), :]
                                ).then_inc(o_hi_ready, 1)

        @block.vector
        def _(dve):
            dve.sem_inc(d_done, D_AHEAD)
            dve.sem_inc(d_added, ADD_AHEAD)
            dve.sem_inc(w_lo_done, LO_AHEAD)
            steps = [0]

            def link(ins):
                steps[0] += 1
                ins.then_inc(setup, 1)
                dve.wait_ge(setup, steps[0])

            def col(c):
                return consts[:, c:c + 1]

            dve.wait_ge(const_in, 48)
            nc.vector.tensor_scalar(mask0[:], ids0[:], col(C_P16), None, ALU.is_equal)
            nc.vector.tensor_scalar(mask2[:], ids2[:], col(C_P32), 0.5, ALU.is_equal, ALU.mult)
            nc.vector.tensor_scalar(mask24[:], ids2[:], 4.0, 0.5, ALU.is_equal,
                                    ALU.mult).then_inc(masks_ready, 1)
            dve.wait_ge(masks_ready, 1)

            def per_seq(ap, n=16):
                return ap.unsqueeze(2).to_broadcast([ap.shape[0], n, S])

            def seqs(ap):
                return ap.rearrange("p (b t) -> p b t", t=S)

            for c in range(TC):
                dve.wait_ge(l0_low_done, c + 1)
                nc.vector.tensor_tensor(seqs(low[:, chunk(c)]), seqs(ps[:, c]),
                                        per_seq(mask0[:, 16 * c:16 * c + 16]),
                                        ALU.mult).then_inc(l0_low_masked, 1)

            def add_to_x(bank, oc, c, done):
                nc.vector.tensor_tensor(x_t[:, oc, chunk(c)], x_t[:, oc, chunk(c)], ps[:, bank],
                                        ALU.add).then_inc(done, 1)

            for c in range(TC):
                for oc in range(KC):
                    dve.wait_ge(l0_done, KC * c + oc + 1)
                    add_to_x((2 + KC * c + oc) % 8, oc, c, l0_added)

            dve.wait_ge(setup_in, 16 * 14)
            nc.vector.tensor_scalar(pos[:], len_tok[:], col(C_M32), None, ALU.add).then_inc(setup, 1)
            steps[0] += 1
            nc.vector.tensor_copy(len_b[:, 0:B], lens[:])
            nc.vector.memset(len_b[:, B:B + 1], 0.0)
            nc.vector.tensor_copy(iota16[:], iota_f[:])
            nc.vector.tensor_scalar(v_rows[:, 0], bt_v[:], float(PSIZE), col(C_M32), ALU.mult, ALU.add)
            nc.vector.tensor_scalar(k_rows[:, 0], bt_k[:], float(P), col(C_P), ALU.mult, ALU.add)
            dve.wait_ge(setup, 1)
            link(nc.vector.tensor_tensor(
                ang[:], pos[:].unsqueeze(2).to_broadcast([P, TT, HD // 2]),
                consts[:, C_FREQ:C_N].unsqueeze(1).to_broadcast([P, TT, HD // 2]), ALU.mult))
            nc.vector.tensor_scalar(v_rows[:, 1], v_rows[:, 0], float(PAGES * PSIZE), None, ALU.add)
            nc.vector.tensor_scalar(k_rows[:, 1], k_rows[:, 0], float(PAGES * P), None, ALU.add)
            link(nc.vector.tensor_scalar(cyc[:], ang[:], 1.0 / TWO_PI, ROUND, ALU.mult, ALU.add))
            link(nc.vector.tensor_scalar(turns[:], cyc[:], ROUND, None, ALU.subtract))
            for part in (PI_A, PI_B, PI_C):
                link(nc.vector.scalar_tensor_tensor(ang[:], turns[:], -part, ang[:], ALU.mult, ALU.add))
            nc.vector.tensor_scalar(ang[:], ang[:], PI_IN, -PI_IN, ALU.min, ALU.max).then_inc(rad_ready, 1)

            def add_l1(b, s):
                dve.wait_ge(l1_done, b + 1)
                cols = x_t[:, :, ds(S * b, S)]
                nc.vector.tensor_tensor(cols, cols, ps[:, 4 + s, 0:KC * S].rearrange("p (k t) -> p k t", k=KC),
                                        ALU.add).then_inc(l1_added, 1)

            def layer2(c):
                dve.wait_ge(l2_low_done, 2 * c + 1)
                nc.vector.tensor_tensor(seqs(low[:, chunk(c)]), seqs(ps[:, 4]),
                                        per_seq(mask2[:, 16 * c:16 * c + 16]), ALU.mult)
                dve.wait_ge(l2_low_done, 2 * c + 2)
                nc.vector.tensor_tensor(seqs(low4[:, chunk(c)]), seqs(ps[0:R2, 5]),
                                        per_seq(mask24[0:R2, 16 * c:16 * c + 16]),
                                        ALU.mult).then_inc(l2_low_masked, 1)
                dve.wait_ge(l2_done, c + 1)
                for oc in range(KC):
                    add_to_x(oc, oc, c, l2_added)
                for kc in range(KC):
                    dve.wait_ge(x_hi_ready, KC * c + kc + 1)
                    nc.vector.tensor_tensor(x_lo[:, kc, chunk(c)], x_t[:, kc, chunk(c)],
                                            x_hi[:, kc, chunk(c)].bitcast(F32),
                                            ALU.subtract).then_inc(x_lo_ready, 1)

            def rope_tables():
                dve.wait_ge(sin_ready, 1)
                link(nc.vector.tensor_tensor(cos_t[:], sin_h[:], sin_h[:], ALU.mult))
                link(nc.vector.tensor_scalar(cos_t[:], cos_t[:], -2.0, 1.0, ALU.mult, ALU.add))
                half = HD // 2
                for n in range(2):
                    for h in range(2):
                        cols = slice(half * h, half * (h + 1))
                        w = norm_w[:, n, cols].unsqueeze(1).to_broadcast([P, TT, half])
                        nc.vector.tensor_tensor(rope_c[:, n, :, cols], cos_t[:], w, ALU.mult)
                        nc.vector.scalar_tensor_tensor(rope_s[:, n, :, cols], sin_t[:], 1.0 - 2.0 * h, w,
                                                       ALU.mult, ALU.mult)

            for c in range(TC):
                with dve.Fori(0, 4) as i:
                    for s in range(4):
                        add_l1(4 * i + (16 * c + s), s)
                if c == 0:
                    rope_tables()
                layer2(c)

            def heads(ap):
                return ap.rearrange("p (h d) -> p h d", h=4)

            def scale_tile(g, m, t, first):
                dve.wait_ge(summed, QKT * g + m + 1)
                dve.wait_ge(rstd_done, QKT * g + m + 1)
                if not (first and t < 2):
                    dve.wait_ge(qk_turned, QKT * g + m - 1)
                p = t % 2
                nc.vector.tensor_tensor(
                    heads(r_out[:, p]), heads(r_cos[:, p]),
                    stat[:, p, RSTD].unsqueeze(2).to_broadcast([P, 4, HD]), ALU.mult).then_inc(rn_done, 1)

            def qk_tile(g, j, t, first, n):
                m = 8 * j + t
                p = t % 2
                dve.wait_ge(sq_done, QKT * g + m + 1)
                nc.vector.tensor_scalar(stat[:, p, VAR], stat[:, p, SQ], 1.0 / HD, EPS,
                                        ALU.mult, ALU.add).then_inc(var_done, 1)
                dve.wait_ge(var_done, QKT * g + m + 1)
                nc.vector.reciprocal(stat[:, p, INV], stat[:, p, VAR]).then_inc(inv_done, 1)
                if not (first and t < 2):
                    dve.wait_ge(rn_done, QKT * g + m - 1)
                for dst, tab in ((r_cos, rope_c), (r_sin, rope_s)):
                    ins = nc.vector.tensor_tensor(heads(dst[:, p]), heads(ps[:, t % 4]),
                                                  tab[:, n, t].unsqueeze(1).to_broadcast([P, 4, HD]), ALU.mult)
                ins.then_inc(roped, 1)
                if not (first and t == 0):
                    scale_tile(g, m - 1, (t - 1) % 8, first and t - 1 < 2)

            def batch_mask(g, b, p, first):
                if not first:
                    dve.wait_ge(max_done, UNITS * g + 4 * b - 4)
                nc.vector.tensor_scalar(mask[:, p, 0:L], iota16[:], len_b[:, ds(b, 1)], NEG,
                                        ALU.is_ge, ALU.mult).then_inc(mask_done, 1)

            def unit_step(g, i, e, c):
                s = 8 * i + e
                p = c % 2
                if 2 <= c < UNITS + 2:
                    dve.wait_ge(exp_done, UNITS * g + s - 1)
                    if c >= 4:
                        dve.wait_ge(o_norm, UNITS * g + s - 3)
                    nc.vector.reciprocal(row_inv[:, p:p + 1], row_sum[:, p:p + 1]).then_inc(inv_l, 1)
                if c < UNITS:
                    b = 2 * i + e // 4
                    if e % 4 == 0:
                        dve.wait_ge(mask_done, (B + 1) * g + b + 1)
                    dve.wait_ge(s_done, UNITS * g + s + 1)
                    settle(dve)
                    nc.vector.tensor_tensor_reduce(
                        out=sm[:, p], in0=ps[:, 2 * p:2 * p + 2].rearrange("p b n -> p (b n)")[:, 0:KEYS],
                        in1=mask[:, e // 4], scale=-SCALE, scalar=BIG, op0=ALU.add, op1=ALU.min,
                        accum_out=sm_min[:, p:p + 1]).then_inc(max_done, 1)
                    if e % 4 == 2:
                        batch_mask(g, b + 1, 1 - e // 4, c < 4)
                if 2 <= c < UNITS + 2:
                    dve.wait_ge(inv_l, UNITS * g + s - 1)
                    dve.wait_ge(pv_done, UNITS * g + s - 1)
                    if c >= 4:
                        dve.wait_ge(o_turned, UNITS * g + s - 3)
                    nc.vector.tensor_scalar(o_sb[:, p], ps[:, 6, 0:P], row_inv[:, p:p + 1], None,
                                            ALU.mult).then_inc(o_norm, 1)
                if 1 <= c <= UNITS:
                    dve.wait_ge(p_turned, UNITS * g + s)
                    if c >= 3:
                        dve.wait_ge(pv_done, UNITS * g + s - 2)
                    nc.vector.tensor_copy(pt[:, 1 - p, 0:PTA * P], ps[:, 4, 0:PTA * P]).then_inc(pt_a, 1)

            with dve.Fori(0, HALVES) as g:
                for t in range(TT):
                    qk_tile(g, 0, t, True, 0)
                with dve.Fori(0, 2) as i:
                    for e in range(2):
                        for t in range(TT):
                            qk_tile(g, 2 * i + (1 + e), t, False, 1)
                scale_tile(g, QKT - 1, 7, False)
                b_done(dve, g)
                settle(dve)
                nc.vector.memset(pr[:, :, KEYS:KPAD], 0.0)
                nc.vector.memset(mask[:, :, L:KEYS], 0.0)
                batch_mask(g, 0, 0, True)
                for c in range(8):
                    unit_step(g, 0, c, c)
                with dve.Fori(1, UNITS // 8) as i:
                    for e in range(8):
                        unit_step(g, i, e, 8 + e)
                for e in range(2):
                    unit_step(g, UNITS // 8, e, UNITS + e)
                with dve.Fori(0, 2) as i:
                    for e in range(2):
                        for c in range(TC):
                            for pair in range(2):
                                dve.wait_ge(o_hi_ready, 16 * g + 8 * i + 4 * e + 2 * c + pair + 1)
                                nc.vector.tensor_tensor(
                                    o_lo[:, pair].rearrange("p h (b t) -> p b h t", t=S),
                                    qk[:, 16 * c:16 * (c + 1), ds(8 * i + (KVH + 4 * e + 2 * pair), 2), :],
                                    o_hi[:, pair].bitcast(F32).rearrange("p h (b t) -> p b h t", t=S),
                                    ALU.subtract).then_inc(o_lo_ready, 1)
                dve.wait_ge(d_done, 16 * g + 16 + D_AHEAD)
                for c in range(TC):
                    for oc in range(KC):
                        add_to_x(KC * c + oc, oc, c, d_added)

        @block.tensor
        def _(pe):
            def mm(o, lhsT, rhs, start, stop):
                return nc.tensor.matmul(o, lhsT, rhs, start=start, stop=stop)

            pe.wait_ge(w0_in, 32)
            for c in range(TC):
                pe.wait_ge(x_in[c], 16)
                for kc in range(KC):
                    ins = mm(ps[:, c], w0b[:, kc], x_t[:, kc, chunk(c)], kc == 0, kc == KC - 1)
                ins.then_inc(l0_low_done, 1)
            for c in range(TC):
                pe.wait_ge(l0_low_masked, TC if c else 1)
                for oc in range(KC):
                    mm(ps[:, (2 + KC * c + oc) % 8], w0a[:, tile(oc)], low[:, chunk(c)], True,
                       True).then_inc(l0_done, 1)

            def expert(b, s):
                pe.wait_ge(exp_in[s], 4 * b + (16 - 4 * s))
                for oc in range(KC):
                    for kc in range(KC):
                        ins = mm(ps[:, 4 + s, S * oc:S * (oc + 1)], w_exp[:, s, kc, tile(oc)],
                                 x_t[:, kc, ds(S * b, S)], kc == 0, kc == KC - 1)
                ins.then_inc(l1_done, 1)

            pe.wait_ge(l0_added, TC * KC)
            for c in range(TC):
                for s in range(4):
                    if c:
                        pe.wait_ge(l2_low_masked, c)
                    expert(16 * c + s, s)
                with pe.Fori(1, 4) as i:
                    for s in range(4):
                        pe.wait_ge(l1_added, 4 * i + (16 * c + s - 3))
                        expert(4 * i + (16 * c + s), s)
                pe.wait_ge(l1_added, 16 * (c + 1))
                if c == 0:
                    pe.wait_ge(w2_in, 16 * 6)
                    pe.wait_ge(l0_added, TC * KC)
                else:
                    pe.wait_ge(l2_added, KC)
                for n, (cols, o) in enumerate(((slice(0, P), ps[:, 4]), (slice(P, N2 * R2), ps[0:R2, 5]))):
                    for kc in range(KC):
                        ins = mm(o, w2a[:, kc, cols], x_t[:, kc, chunk(c)], kc == 0, kc == KC - 1)
                    ins.then_inc(l2_low_done, 1)
                for oc in range(KC):
                    for kc in range(KC):
                        mm(ps[:, oc], w2[:, kc, tile(oc)], x_t[:, kc, chunk(c)], kc == 0, False)
                pe.wait_ge(l2_low_masked, c + 1)
                for oc in range(KC):
                    mm(ps[:, oc], w2b[:, tile(oc)], low[:, chunk(c)], False, False)
                    ins = mm(ps[:, oc], w2b[0:R2, tile(oc)], low4[:, chunk(c)], False, True)
                ins.then_inc(l2_done, 1)
            pe.wait_ge(x_lo_ready, TC * KC)

            def project(t, par):
                for kc in range(KC):
                    for n, (x, w) in enumerate(((x_hi, w_hi), (x_hi, w_lo), (x_lo, w_hi))):
                        ins = mm(ps[:, t % 4], x[:, kc, tile(t)], w[par][:, chunk(kc)],
                                 kc == 0 and n == 0, kc == KC - 1 and n == 2)
                ins.then_inc(proj_done, 1)

            def turn_qk(g, m, t, first):
                pe.wait_ge(rn_done, QKT * g + m + 1)
                if not (first and t < 2):
                    pe.wait_ge(qk_stored, QKT * g + m - 1)
                for h in range(4):
                    ins = nc.tensor.transpose(ps[:, 4 + t % 2, tile(h)], r_out[:, t % 2, tile(h)], ident)
                ins.then_inc(qk_turned, 1)

            def block_of(g, j, par, first):
                pe.wait_ge(w_lo_done, 4 * (NBLK * g + j) + 4 + LO_AHEAD)
                for t in range(TT):
                    m = 8 * j + t
                    if not (first and t < 4):
                        pe.wait_ge(roped, QKT * g + m - 3)
                    project(t, par)
                    if t >= 2:
                        turn_qk(g, m - 2, t - 2, first)
                    elif not first:
                        turn_qk(g, m - 2, t + 6, False)

            def scores(g, s, c, e):
                p, b2, k = c % 2, e // 4, e % 4
                if k == 0:
                    pe.wait_ge(q_in[b2], 16 * nth[0] + 16)
                    pe.wait_ge(k_in[b2], 16 * SPP * nth[0] + 16 * SPP)
                    pe.wait_ge(k_in2[b2], 16 * PPP * nth[0] + 16 * PPP)
                if c >= 2:
                    pe.wait_ge(max_done, UNITS * g + s - 1)
                q = qk_st[:, b2, KVH + REP * k:KVH + REP * (k + 1), :].rearrange("p h t -> p (h t)")
                mm(ps[:, 2 * p], q, k_buf[:, b2, :, k, :], True, True)
                mm(ps[:, 2 * p + 1, 0:S], q, qk_st[:, b2, k], True, True).then_inc(s_done, 1)

            def values(g, s, c, e):
                p, b2, k = c % 2, e // 4, e % 4
                pe.wait_ge(pt_a, UNITS * g + s + 1)
                pe.wait_ge(pt_b, UNITS * g + s + 1)
                if k == 0:
                    pe.wait_ge(v_in[b2], 16 * VCH * nth_v[0] + 16 * VCH)
                    pe.wait_ge(vn_in[b2], 16 * nth_v[0] + 16)
                if c >= 1:
                    pe.wait_ge(o_norm, UNITS * g + s)
                for ch in range(KCH):
                    ins = mm(ps[:, 6, 0:P], pt[:, p, tile(ch)], v_buf[:, b2, ch, HD * k:HD * (k + 1)],
                             ch == 0, ch == KCH - 1)
                ins.then_inc(pv_done, 1)

            def turn_o(g, s, c, e, b):
                pe.wait_ge(o_norm, UNITS * g + s + 1)
                if e % 4 == 0 and c >= 4:
                    pe.wait_ge(o_stored, B * g + b)
                nc.tensor.transpose(ps[:, 7, tile(e % 4)], o_sb[:, c % 2], ident).then_inc(o_turned, 1)

            def turn_p(g, s, c):
                pe.wait_ge(exp_done, UNITS * g + s + 1)
                if c >= 1:
                    pe.wait_ge(pt_a, UNITS * g + s)
                    pe.wait_ge(pt_b, UNITS * g + s)
                for ch in range(KCH):
                    o = ps[:, 4, tile(ch)] if ch < PTA else ps[:, 5, tile(ch - PTA)]
                    ins = nc.tensor.transpose(o, pr[:, c % 2, tile(ch)], ident)
                ins.then_inc(p_turned, 1)

            nth, nth_v = [0], [0]

            def unit_step(g, i, e, c):
                s = 8 * i + e
                nth[0] = 16 * g + i
                nth_v[0] = 16 * g + i + (0 if e >= 2 else -1)
                if c < UNITS:
                    scores(g, s, c, e)
                if 2 <= c < UNITS + 2:
                    values(g, s - 2, c - 2, (e - 2) % 8)
                if 3 <= c:
                    turn_o(g, s - 3, c - 3, (e - 3) % 8, 2 * i + (e - 3) // 4)
                if 1 <= c <= UNITS:
                    turn_p(g, s - 1, c - 1)

            with pe.Fori(0, HALVES) as g:
                pe.wait_ge(d_added, 8 * g + ADD_AHEAD)
                block_of(g, 0, 0, True)
                with pe.Fori(0, 2) as i:
                    for e in range(2):
                        block_of(g, 2 * i + (1 + e), 1 - e, False)
                pe.wait_ge(w_lo_done, 4 * (NBLK * g + 5) + 4 + LO_AHEAD)
                for t in range(TT):
                    if t < 4:
                        pe.wait_ge(roped, QKT * g + QKT + t - 3)
                    else:
                        pe.wait_ge(v_copied, 8 * g + t - 3)
                    project(t, 1)
                    if t < 2:
                        turn_qk(g, QKT - 2 + t, 6 + t, False)
                for c in range(8):
                    unit_step(g, 0, c, c)
                with pe.Fori(1, UNITS // 8) as i:
                    for e in range(8):
                        unit_step(g, i, e, 8 + e)
                for e in range(3):
                    unit_step(g, UNITS // 8, e, UNITS + e)
                for q in range(OBLK):
                    par = q % 2
                    pe.wait_ge(w_lo_done, 4 * (NBLK * g + BLK + q) + 4 + LO_AHEAD)
                    for c in range(TC):
                        for pair in range(2):
                            pe.wait_ge(o_lo_ready, 16 * g + 4 * q + 2 * c + pair + 1)
                            for h in range(2):
                                for oc in range(KC):
                                    cols = slice(512 * (2 * pair + h) + P * oc, 512 * (2 * pair + h) + P * (oc + 1))
                                    for n, (w, o) in enumerate(((w_hi, o_hi), (w_hi, o_lo), (w_lo, o_hi))):
                                        ins = mm(ps[:, KC * c + oc], w[par][:, cols], o[:, pair, h],
                                                 q == 0 and pair == 0 and h == 0 and n == 0,
                                                 q == OBLK - 1 and pair == 1 and h == 1 and n == 2)
                            ins.then_inc(d_done, 1)


def kernel(x, itok_B_3_7, itok_B_0_15, itok_B_0_2, itok_Bx16_0_63, itok_B_207_1644,
           L0_cond_A, L0_cond_B, L1_cond_weight, L2_cond_W, L2_cond_lora_A, L2_cond_lora_B_w,
           L3_cond_Wq, L3_cond_Wk, L3_cond_Wv, L3_cond_Wo, L3_cond_q_norm_w, L3_cond_k_norm_w,
           L3_cond_k_cache, L3_cond_v_cache):
    import numpy as np
    import concourse.bacc as bacc
    from concourse.bass_utils import run_bass_kernel_spmd

    def fold(w):
        w = np.asarray(w)
        return w.reshape(w.shape[0], KC, P).transpose(2, 1, 0)

    def blocks(w, g, n):
        w = np.asarray(w)[g * n * 512:(g + 1) * n * 512]
        return [fold(w[512 * j:512 * (j + 1)]).reshape(P, BW) for j in range(n)]

    wo = np.asarray(L3_cond_Wo).reshape(DM, HALVES, OBLK, 4, HD).transpose(1, 2, 4, 3, 0)
    l3_w = []
    for g in range(HALVES):
        l3_w += blocks(L3_cond_Wk, g, 1) + blocks(L3_cond_Wq, g, OBLK) + blocks(L3_cond_Wv, g, 1)
        l3_w += [wo[g, j].reshape(P, BW) for j in range(OBLK)]
    kc = np.asarray(L3_cond_k_cache).reshape(PAGES, PSIZE, HALVES, KVH, HD).transpose(2, 0, 4, 3, 1)
    kc = np.ascontiguousarray(kc)
    vc = np.asarray(L3_cond_v_cache).reshape(PAGES, PSIZE, HALVES, KVH * HD).transpose(2, 0, 1, 3)
    const = np.zeros((P, C_N), np.float32)
    rows = np.arange(P)
    const[:, C_ID:C_ID + P] = np.eye(P)
    const[:, C_P16], const[:, C_P32], const[:, C_M32], const[:, C_P] = rows // R0, rows // R2, rows % S, rows
    const[:, C_FREQ:] = 1.0 / 10000.0 ** (np.arange(0, HD, 2) / HD)
    lora_a = np.asarray(L2_cond_lora_A)
    lens, pages = np.asarray(itok_B_207_1644), np.asarray(itok_Bx16_0_63)
    arrays = {
        "lens_q": lens.reshape(TT, BPT).T, "pages_q": pages.reshape(B, VCH, P // PSIZE).transpose(2, 0, 1),
        "pages_k": pages[:, SPP:],
        "x_t": fold(np.asarray(x).reshape(T, DM)),
        "ids0": itok_B_3_7, "ids1": itok_B_0_15, "ids2": itok_B_0_2,
        "pages": pages, "lens": lens,
        "l0_b": fold(np.asarray(L0_cond_B).reshape(N0 * R0, DM)),
        "l0_a": np.asarray(L0_cond_A).transpose(0, 2, 1).reshape(N0 * R0, DM),
        "l1_w": np.asarray(L1_cond_weight).reshape(16, DM, KC, P).transpose(0, 3, 2, 1),
        "l2_w": fold(L2_cond_W),
        "l2_a": fold(lora_a.transpose(0, 2, 1).reshape(N2 * R2, DM)),
        "l2_b": np.asarray(L2_cond_lora_B_w).T,
        "l3_w": np.stack(l3_w),
        "k_norm": L3_cond_k_norm_w, "q_norm": L3_cond_q_norm_w,
        "k_t": kc.reshape(HALVES * PAGES, HD, KVH, PSIZE),
        "k_rows": kc.reshape(HALVES * PAGES * HD, KVH * PSIZE),
        "v_rows": vc.reshape(HALVES * PAGES * PSIZE, KVH * HD),
        "consts": const, "iota": np.arange(L, dtype=np.float32),
    }
    arrays = {f"in_{n}": np.ascontiguousarray(v) for n, v in arrays.items()}
    nc = bacc.Bacc("TRN2", target_bir_lowering=False, num_devices=1)
    a = {n[3:]: nc.dram_tensor(n, v.shape, mybir.dt.from_np(v.dtype), kind="ExternalInput").ap()
         for n, v in arrays.items()}
    a["v_new"] = nc.dram_tensor("v_new_dram", [HALVES * B, S, KVH * HD], F32, kind="Internal").ap()
    out = nc.dram_tensor("out_t", [P, KC, T], F32, kind="ExternalOutput").ap()
    build(nc, a, out)
    r = run_bass_kernel_spmd(nc, [arrays], core_ids=[0])
    got = np.asarray(r.results[0]["out_t"])
    return np.ascontiguousarray(got.transpose(2, 1, 0).reshape(B, S, DM))
```

```python
from contextlib import ExitStack

import concourse.bass as bass
from concourse import mybir

F32 = mybir.dt.float32
F32R = mybir.dt.float32r
BF16 = mybir.dt.bfloat16
F16 = mybir.dt.float16
I32 = mybir.dt.int32
I16 = mybir.dt.int16
ALU = mybir.AluOpType
ACT = mybir.ActivationFunctionType
ds = bass.ds

P = 128
B, S, DM = 32, 32, 512
T = B * S
KC = DM // P
TC = T // 512
TT = T // P
BPT = P // S
BPC = 512 // S
HD = 128
HQ, HK = 32, 8
REP = HQ // HK
HALVES = 2
KVH = HK // HALVES
QH = HQ // HALVES
PAGES, PSIZE, NPP = 64, 32, 16
L = NPP * PSIZE
KEYS = L + S
KPAD = 640
KCH = KPAD // P
VCH = L // P
SLOTS = KVH + QH
BLK = 6
OBLK = 4
NBLK = BLK + OBLK
BW = KC * 512
QKT = 5 * TT
UNITS = B * KVH
SPP = 13
PPP = NPP - SPP
PIECES = 8
PW = BW // PIECES
TLAG = 3
PTA = 2
R0, N0 = 16, 8
R2, N2 = 32, 5
EPS = 1e-6
SCALE = HD ** -0.5
NEG = -1e30
BIG = 3e38
TWO_PI = 6.283185307179586
ROUND = 1.5 * 2.0 ** 23
PI_A = 6.28125
PI_B = 0.0019350051879882812
PI_C = TWO_PI - PI_A - PI_B
PI_IN = 3.1415925
C_ID, C_P16, C_P32, C_M32, C_P, C_FREQ = 0, 128, 129, 130, 131, 132
C_N = C_FREQ + HD // 2


def build(nc, a, out):
    with ExitStack() as ctx:
        def sb(name, shape, dt=F32):
            return ctx.enter_context(nc.sbuf_tensor(name, shape, dt))

        def sem(name):
            return ctx.enter_context(nc.semaphore(name))

        x_t = sb("x_t", [P, KC, T])
        x_hi = sb("x_hi", [P, KC, T], F32R)
        x_lo = sb("x_lo", [P, KC, T], F32R)
        rope_c = sb("rope_c", [P, 2, TT, HD])
        rope_s = sb("rope_s", [P, 2, TT, HD])
        consts = sb("consts_sb", [P, C_N])
        ident = consts[:, C_ID:C_ID + P]
        iota16 = sb("iota16", [P, L], F16)
        len_b = sb("len_b", [P, B + 1])
        v_rows = sb("v_rows", [P, HALVES, B, VCH], I16)
        k_rows = sb("k_rows", [P, HALVES, B, PPP], I16)
        v_idx = sb("v_idx", [P, 2, VCH], I32)
        k_idx = sb("k_idx", [P, 2, PPP], I32)
        ids_row = sb("ids_row", [1, B], I32)
        pages_row = sb("pages_row", [1, B, NPP], I32)
        stat = sb("stat", [P, 2, 6, 4])
        SQ, VAR, INV, Y0, NT, RSTD = range(6)
        sm_min = sb("sm_min", [P, 2])
        row_sum = sb("row_sum", [P, 2])
        row_inv = sb("row_inv", [P, 2])
        at = [-(-nc.sbuf_base // 32) * 32]

        def place(name, shape, dt=F32, p=P):
            t = nc.alloc_sbuf_tensor_at(name, [p] + shape, dt, offset=at[0])
            size = mybir.dt.size(dt)
            for n in shape:
                size *= n
            at[0] += -(-size // 32) * 32
            return t

        store_at = at[0]
        qk = place("qk", [B, SLOTS, S])
        region = at[0]
        at[0] = store_at
        ids0 = place("ids0", [B], I32)
        ids2 = place("ids2", [B], I32)
        mask0 = place("mask0", [B])
        mask2 = place("mask2", [B])
        mask24 = place("mask24", [B])
        lens = place("lens", [B], I32)
        len_tok = place("len_tok", [TT], I32)
        pos = place("pos", [TT])
        bt_v = place("bt_v", [B, VCH], I32)
        bt_k = place("bt_k", [B, PPP], I32)
        norm_w = place("norm_w", [2, HD])
        iota_f = place("iota_f", [L])
        ang = place("ang", [TT, HD // 2])
        cyc = place("cyc", [TT, HD // 2])
        turns = place("turns", [TT, HD // 2])
        sin_t = place("sin_t", [TT, HD // 2])
        sin_h = place("sin_h", [TT, HD // 2])
        cos_t = place("cos_t", [TT, HD // 2])
        at[0] = region
        w_exp = place("w_exp", [4, KC, DM])
        w0b = place("w0b", [KC, P])
        w0a = place("w0a", [DM])
        w2 = place("w2", [KC, DM])
        w2a = place("w2a", [KC, N2 * R2])
        w2b = place("w2b", [DM])
        low = place("low", [T])
        low4 = place("low4", [T], p=R2)
        at[0] = region
        w_in = place("w_in", [BW])
        w_hi0, w_lo0 = place("w_hi0", [BW], F32R), place("w_lo0", [BW], F32R)
        w_hi1, w_lo1 = place("w_hi1", [BW], F32R), place("w_lo1", [BW], F32R)
        w_hi, w_lo = (w_hi0, w_hi1), (w_lo0, w_lo1)
        work = at[0]
        r_sin = place("r_sin", [2, 512])
        r_cos = place("r_cos", [2, 512])
        r_out = place("r_out", [2, 512])
        b_sq = place("b_sq", [512])
        at[0] = work
        v_out = place("v_out", [TT, 512])
        at[0] = work
        o_hi = place("o_hi", [2, 2, 512], F32R)
        o_lo = place("o_lo", [2, 2, 512], F32R)
        at[0] = region
        k_buf, v_buf, qk_st = [None] * 2, [None] * 2, [None] * 2
        for p in range(2):
            k_buf[p] = place(f"k_buf{p}", [NPP + 1, KVH, S])
            v_buf[p] = place(f"v_buf{p}", [KCH, KVH * HD])
            qk_st[p] = place(f"qk_st{p}", [QH, S])
            if p == 0:
                assert at[0] <= region + 3 * 4 * BW
                sm = place("sm", [2, KEYS])
                pr = place("pr", [2, KPAD])
                pt = place("pt", [2, KPAD])
                o_sb = place("o_sb", [2, P])
                mask = place("mask", [2, KEYS], BF16)
                assert at[0] <= work
        KA = NPP // 2 + 1
        SC = 512 - KA * S

        ps = ctx.enter_context(nc.psum_tensor("ps", [P, 8, 512], F32))

        ids_in, const_in, setup_in = sem("ids_in"), sem("const_in"), sem("setup_in")
        x_in = [sem(f"x_in{c}") for c in range(TC)]
        w0b_in, w0a_in, w2_in = sem("w0b_in"), sem("w0a_in"), sem("w2_in")
        exp_in = [sem(f"exp_in{s}") for s in range(4)]
        w_in_done = sem("w_in_done")
        q_in = [sem(f"q_in{p}") for p in range(2)]
        k_in = [sem(f"k_in{p}") for p in range(2)]
        k_in2 = [sem(f"k_in2{p}") for p in range(2)]
        v_in = [sem(f"v_in{p}") for p in range(2)]
        vn_in = [sem(f"vn_in{p}") for p in range(2)]
        v_stored = sem("v_stored")
        out_stored = sem("out_stored")
        settled = sem("settled")
        setup = sem("setup")
        masks_ready = sem("masks_ready")
        rad_ready, sin_ready = sem("rad_ready"), sem("sin_ready")
        l0_low_done, l0_low_masked, l0_done, l0_added = (
            sem("l0_low_done"), sem("l0_low_masked"), sem("l0_done"), sem("l0_added"))
        l1_done, l1_added = sem("l1_done"), sem("l1_added")
        l2_low_done, l2_low4_masked, l2_low_masked, l2_done, l2_added = (
            sem("l2_low_done"), sem("l2_low4_masked"), sem("l2_low_masked"), sem("l2_done"), sem("l2_added"))
        x_hi_ready, x_lo_ready = sem("x_hi_ready"), sem("x_lo_ready")
        w_hi_done, w_lo_done = sem("w_hi_done"), sem("w_lo_done")
        proj_done, sq_done, var_done, inv_done, y0_done = (
            sem("proj_done"), sem("sq_done"), sem("var_done"), sem("inv_done"), sem("y0_done"))
        newton, rstd_done, roped, summed, rn_done = (
            sem("newton"), sem("rstd_done"), sem("roped"), sem("summed"), sem("rn_done"))
        qk_turned, qk_stored, v_copied = sem("qk_turned"), sem("qk_stored"), sem("v_copied")
        v_padded, idx_copied, mask_done = sem("v_padded"), sem("idx_copied"), sem("mask_done")
        s_done, max_done, exp_done, p_turned = (
            sem("s_done"), sem("max_done"), sem("exp_done"), sem("p_turned"))
        pt_a, pt_b, pv_done, inv_l, o_norm, o_turned, o_stored = (
            sem("pt_a"), sem("pt_b"), sem("pv_done"), sem("inv_l"), sem("o_norm"),
            sem("o_turned"), sem("o_stored"))
        o_hi_ready, o_lo_ready, d_done, d_added = (
            sem("o_hi_ready"), sem("o_lo_ready"), sem("d_done"), sem("d_added"))
        L1_AHEAD = 8
        D_AHEAD, ADD_AHEAD, LO_AHEAD = 8, 8, PIECES

        block = ctx.enter_context(nc.Block())

        def chunk(c):
            return slice(512 * c, 512 * (c + 1))

        def piece(q):
            return slice(PW * q, PW * (q + 1))

        def pieces_at(t):
            first, last = round(PIECES * max(t - 1, 0) / 6), round(PIECES * min(t, 6) / 6)
            return range(first, last)

        def tile(t):
            return slice(P * t, P * (t + 1))

        def b_done(eng, g):
            eng.wait_ge(v_stored, 8 * TT * g + 8 * TT)

        def settle(eng):
            eng.sem_inc(settled, 1)

        @block.sync
        def _(sp):
            sp.dma_start(ids_row[:], a["ids1"].unsqueeze(0)).then_inc(ids_in, 16)
            sp.dma_start(w0b[:], a["l0_b"]).then_inc(w0b_in, 16)
            sp.dma_start(x_t[:, :, chunk(0)], a["x_t"][:, :, chunk(0)]).then_inc(x_in[0], 16)
            sp.dma_start(w0a[:], a["l0_a"]).then_inc(w0a_in, 16)
            sp.dma_start(x_t[:, :, chunk(1)], a["x_t"][:, :, chunk(1)]).then_inc(x_in[1], 16)
            sp.wait_ge(ids_in, 16)

            def load_expert(b, s):
                e = sp.value_load(ids_row[0:1, ds(b, 1)], min_val=0, max_val=15)
                if not isinstance(b, int):
                    sp.wait_ge(l1_done, b - 3)
                sp.dma_start(w_exp[:, s], a["l1_w"][ds(e, 1)].rearrange("e p k n -> p (e k) n")
                             ).then_inc(exp_in[s], 16)

            for s in range(4):
                load_expert(s, s)
            sp.dma_start(w2[:], a["l2_w"]).then_inc(w2_in, 16)
            sp.dma_start(w2a[:], a["l2_a"]).then_inc(w2_in, 16)
            for r in range(P // R2):
                sp.dma_start(w2b[R2 * r:R2 * (r + 1)], a["l2_b"]).then_inc(w2_in, 16)
            with sp.Fori(1, B // 4) as i:
                for s in range(4):
                    load_expert(4 * i + s, s)
            sp.wait_ge(l1_done, B)

            def load_block(n):
                sp.wait_ge(w_lo_done, PIECES * n + LO_AHEAD)
                sp.dma_start(w_in[:], a["l3_w"][ds(n, 1)].rearrange("n p w -> p (n w)")
                             ).then_inc(w_in_done, 16)

            def load_cached(g, b, p, free=None):
                settle(sp)
                pages = nc.values_load_multi_w_load_instructions(
                    pages_row[0:1, ds(b, 1), 0:SPP], engines=[mybir.EngineType.SP], min_val=0,
                    max_val=PAGES - 1, skip_runtime_bounds_check_because="ids of cache pages")[1]
                if free is not None:
                    sp.wait_ge(s_done, free)
                for j in range(SPP):
                    sp.dma_start(
                        k_buf[p][:, j],
                        a["k_t"][ds(PAGES * g + pages[j], 1)].rearrange("n p h t -> p (n h) t")
                    ).then_inc(k_in[p], 16)

            def load_new(b, p):
                sp.dma_start(qk_st[p][:], qk[:, ds(b, 1), KVH:SLOTS].rearrange("p b h t -> p (b h) t")
                             ).then_inc(q_in[p], 16)
                sp.dma_start(k_buf[p][:, NPP], qk[:, ds(b, 1), 0:KVH].rearrange("p b h t -> p (b h) t")
                             ).then_inc(q_in[p], 16)

            def load_values(g, b, p, first):
                if first:
                    sp.wait_ge(v_padded, 2 * g + (p + 1))
                    settle(sp)
                    b_done(sp, g)
                else:
                    sp.wait_ge(pv_done, UNITS * g + 4 * b - 4)
                settle(sp)
                sp.dma_start(v_buf[p][0:S, VCH], a["v_new"][ds(B * g + b, 1)].rearrange("n t w -> (n t) w")
                             ).then_inc(vn_in[p], 16)

            with sp.Fori(0, HALVES) as g:
                with sp.Fori(0, BLK) as j:
                    load_block(NBLK * g + j)

                def store_v(t):
                    sp.wait_ge(v_copied, 8 * g + (t + 2))
                    settle(sp)
                    sp.dma_start(
                        a["v_new"][ds(B * g + BPT * t, 2 * BPT)].rearrange("(u n) t w -> (n t) u w", u=2),
                        v_out[:, t:t + 2]).then_inc(v_stored, 16)

                sp.wait_ge(proj_done, 48 * g + QKT)
                sp.wait_ge(w_lo_done, PIECES * (NBLK * g + BLK) + LO_AHEAD)
                load_cached(g, 0, 0)
                sp.wait_ge(qk_stored, QKT * g + QKT)
                settle(sp)
                load_new(0, 0)
                for t in range(0, TT, 2):
                    store_v(t)
                load_values(g, 0, 0, True)
                load_cached(g, 1, 1)
                load_new(1, 1)
                load_values(g, 1, 1, True)
                with sp.Fori(1, B // 2) as i:
                    for p in range(2):
                        b = 2 * i + p
                        load_cached(g, b, p, free=UNITS * g + 4 * b - 4)
                        load_new(b, p)
                        load_values(g, b, p, False)
                sp.wait_ge(s_done, UNITS * (g + 1) - KVH)
                settle(sp)
                with sp.Fori(BLK, NBLK) as j:
                    load_block(NBLK * g + j)
            for c in range(TC):
                for oc in range(KC):
                    sp.wait_ge(d_added, ADD_AHEAD + 8 * (HALVES - 1) + KC * c + oc + 1)
                    sp.dma_start(out[:, oc, chunk(c)], x_t[:, oc, chunk(c)]).then_inc(out_stored, 16)
            sp.wait_ge(out_stored, 16 * TC * KC)

        @block.gpsimd
        def _(pool):
            def split_low(j, part):
                n, par = j
                cols = piece(part)
                pool.wait_ge(w_hi_done, PIECES * n + (part + 1))
                nc.gpsimd.tensor_tensor(w_lo[par][:, cols], w_in[:, cols],
                                        w_hi[par][:, cols].bitcast(F32),
                                        ALU.subtract).then_inc(w_lo_done, 1)

            def qk_tile(g, j, t, first, par):
                m = 8 * j + t
                for part in pieces_at(t):
                    split_low((NBLK * g + j + 1, 1 - par), part)
                pool.wait_ge(roped, QKT * g + m + 1)
                c4 = r_cos[:, t % 2].rearrange("p (h d) -> p h d", h=4)
                s4 = r_sin[:, t % 2].rearrange("p (h d) -> p h d", h=4)
                half = HD // 2
                nc.gpsimd.tensor_tensor(c4[:, :, 0:half], c4[:, :, 0:half], s4[:, :, half:HD], ALU.add)
                nc.gpsimd.tensor_tensor(c4[:, :, half:HD], c4[:, :, half:HD], s4[:, :, 0:half],
                                        ALU.add).then_inc(summed, 1)

            def fetch(g, b, p, first):
                if not first:
                    pool.wait_ge(s_done, UNITS * g + 4 * b - 4)
                n = B * g + b
                row = k_rows[:, :].rearrange("p g b c -> p (g b) c")
                nc.gpsimd.tensor_copy(k_idx[:, p], row[:, ds(n, 1)]).then_inc(idx_copied, 1)
                pool.wait_ge(idx_copied, 2 * n + 1)
                settle(pool)
                for j in range(PPP):
                    pool.indirect_dma_start(
                        k_buf[p][:, SPP + j].rearrange("p h t -> p (h t)"), None, a["k_rows"],
                        bass.IndirectOffsetOnAxis(k_idx[:, p, j:j + 1], 0)).then_inc(k_in2[p], 16)
                if not first:
                    pool.wait_ge(pv_done, UNITS * g + 4 * b - 4)
                row = v_rows[:, :].rearrange("p g b c -> p (g b) c")
                nc.gpsimd.tensor_copy(v_idx[:, p], row[:, ds(n, 1)]).then_inc(idx_copied, 1)
                pool.wait_ge(idx_copied, 2 * n + 2)
                settle(pool)
                for c in range(VCH):
                    pool.indirect_dma_start(
                        v_buf[p][:, c], None, a["v_rows"],
                        bass.IndirectOffsetOnAxis(v_idx[:, p, c:c + 1], 0)).then_inc(v_in[p], 16)

            with pool.Fori(0, HALVES) as g:
                for part in range(PIECES):
                    split_low((NBLK * g, 0), part)
                for t in range(TT):
                    qk_tile(g, 0, t, True, 0)
                with pool.Fori(0, 2) as i:
                    for e in range(2):
                        for t in range(TT):
                            qk_tile(g, 2 * i + (1 + e), t, False, 1 - e)
                for p in range(2):
                    if p == 0:
                        pool.wait_ge(proj_done, 48 * g + QKT)
                    else:
                        b_done(pool, g)
                    settle(pool)
                    nc.gpsimd.memset(v_buf[p][:, VCH], 0.0).then_inc(v_padded, 1)
                    fetch(g, p, p, True)
                with pool.Fori(1, B // 2) as i:
                    for p in range(2):
                        fetch(g, 2 * i + p, p, False)
                for q in range(OBLK):
                    if q == 0:
                        pool.wait_ge(pv_done, UNITS * (g + 1) - KVH)
                    for part in range(PIECES):
                        if q == 0 and part >= PIECES - 3:
                            pool.wait_ge(exp_done, UNITS * (g + 1) - (part < PIECES - 1))
                        split_low((NBLK * g + BLK + q, q % 2), part)

        @block.scalar
        def _(act):
            act.dma_start(consts[:], a["consts"]).then_inc(const_in, 16)
            act.dma_start(ids0[:], a["ids0"].partition_broadcast(P)).then_inc(const_in, 16)
            act.dma_start(ids2[:], a["ids2"].partition_broadcast(P)).then_inc(const_in, 16)
            act.dma_start(lens[:], a["lens"].partition_broadcast(P)).then_inc(setup_in, 16)
            for q in range(4):
                rows = slice(32 * q, 32 * (q + 1))
                act.dma_start(len_tok[rows], a["lens_q"][q].partition_broadcast(S)).then_inc(setup_in, 16)
                act.dma_start(bt_v[rows], a["pages_q"][q].partition_broadcast(PSIZE)).then_inc(setup_in, 16)
            act.dma_start(bt_k[:], a["pages_k"].partition_broadcast(P)).then_inc(setup_in, 16)
            act.dma_start(norm_w[:, 0], a["k_norm"].partition_broadcast(P)).then_inc(setup_in, 16)
            act.dma_start(norm_w[:, 1], a["q_norm"].partition_broadcast(P)).then_inc(setup_in, 16)
            act.dma_start(iota_f[:], a["iota"].partition_broadcast(P)).then_inc(setup_in, 16)
            act.dma_start(pages_row[:], a["pages"].unsqueeze(0)).then_inc(setup_in, 16)
            act.wait_ge(rad_ready, 1)
            nc.scalar.activation(sin_t[:], ang[:], ACT.Sin)
            nc.scalar.activation(sin_h[:], ang[:], ACT.Sin, scale=0.5).then_inc(sin_ready, 1)
            for kc in range(KC):
                act.wait_ge(l2_added, kc + 1)
                nc.scalar.copy(x_hi[:, kc, chunk(0)], x_t[:, kc, chunk(0)]).then_inc(x_hi_ready, 1)

            def split_high(n, par, part):
                cols = piece(part)
                if part == 0:
                    act.wait_ge(w_in_done, 16 * n + 16)
                nc.scalar.copy(w_hi[par][:, cols], w_in[:, cols]).then_inc(w_hi_done, 1)

            def store_qk(g, m, j, t):
                act.wait_ge(qk_turned, QKT * g + m + 1)
                nc.scalar.copy(
                    qk[:, BPT * t:BPT * (t + 1), ds(4 * j, 4), :],
                    ps[:, 4 + t % 2].rearrange("p (h b s) -> p b h s", h=4, b=BPT)
                ).then_inc(qk_stored, 1)

            def qk_tile(g, j, t, first, par):
                m = 8 * j + t
                for part in pieces_at(t):
                    split_high(NBLK * g + j + 1, 1 - par, part)
                act.wait_ge(proj_done, 48 * g + m + 1)
                if not (first and t == 0):
                    act.wait_ge(sq_done, QKT * g + m)
                for h in range(4):
                    ins = nc.scalar.activation(b_sq[:, tile(h)], ps[:, t % 4, tile(h)], ACT.Square,
                                               accum_out=stat[:, t % 2, SQ, h:h + 1])
                ins.then_inc(sq_done, 1)
                act.wait_ge(inv_done, QKT * g + m + 1)
                if not (first and t < 2):
                    act.wait_ge(rstd_done, QKT * g + m - 1)
                nc.scalar.activation(stat[:, t % 2, Y0], stat[:, t % 2, INV], ACT.Sqrt).then_inc(y0_done, 1)
                if t >= TLAG:
                    store_qk(g, m - TLAG, j, t - TLAG)
                elif not first:
                    store_qk(g, m - TLAG, j - 1, t - TLAG + TT)

            def exp_unit(g, s, c):
                act.wait_ge(max_done, UNITS * g + s + 1)
                if c >= 2:
                    act.wait_ge(p_turned, UNITS * g + s - 1)
                nc.scalar.activation(pr[:, c % 2, 0:KEYS], sm[:, c % 2], ACT.Exp,
                                     bias=sm_min[:, c % 2:c % 2 + 1], scale=-1.0,
                                     accum_out=row_sum[:, c % 2:c % 2 + 1]).then_inc(exp_done, 1)

            def copy_pt(g, s, c):
                act.wait_ge(p_turned, UNITS * g + s + 1)
                if c >= 2:
                    act.wait_ge(pv_done, UNITS * g + s - 1)
                nc.scalar.copy(pt[:, c % 2, PTA * P:KPAD], ps[:, 5, 0:KPAD - PTA * P]).then_inc(pt_b, 1)

            def store_o(g, b, s):
                act.wait_ge(o_turned, UNITS * g + s + 1)
                nc.scalar.copy(qk[:, ds(b, 1), KVH:SLOTS, :].rearrange("p b h t -> p (b h t)"),
                               ps[:, 7, :]).then_inc(o_stored, 1)

            def unit_step(g, i, e, c):
                s = 8 * i + e
                if c < UNITS:
                    exp_unit(g, s, c)
                if c >= 6 and c % 4 == 2:
                    store_o(g, 2 * i + (e // 4 - 1), s - 3)
                if 1 <= c <= UNITS:
                    copy_pt(g, s - 1, c - 1)

            with act.Fori(0, HALVES) as g:
                act.wait_ge(d_done, 16 * g + 4)
                for part in range(PIECES):
                    split_high(NBLK * g, 0, part)
                for t in range(TT):
                    qk_tile(g, 0, t, True, 0)
                with act.Fori(0, 2) as i:
                    for e in range(2):
                        for t in range(TT):
                            qk_tile(g, 2 * i + (1 + e), t, False, 1 - e)
                for t in range(TT):
                    if t < TLAG:
                        store_qk(g, QKT - TLAG + t, 4, TT - TLAG + t)
                    if t < 2:
                        act.wait_ge(summed, QKT * g + QKT - 1 + t)
                    elif t < 4:
                        act.wait_ge(rn_done, QKT * g + QKT - 3 + t)
                    act.wait_ge(proj_done, 48 * g + QKT + t + 1)
                    nc.scalar.copy(v_out[:, t], ps[:, t % 4]).then_inc(v_copied, 1)
                for c in range(8):
                    unit_step(g, 0, c, c)
                with act.Fori(1, UNITS // 8) as i:
                    for e in range(8):
                        unit_step(g, i, e, 8 + e)
                unit_step(g, UNITS // 8, 0, UNITS)

                def o_high(q, c, pair):
                    nc.scalar.copy(
                        o_hi[:, pair].rearrange("p h (b t) -> p b h t", t=S),
                        qk[:, 16 * c:16 * (c + 1), KVH + 4 * q + 2 * pair:KVH + 4 * q + 2 * pair + 2, :]
                    ).then_inc(o_hi_ready, 1)

                act.wait_ge(pv_done, UNITS * (g + 1) - KVH)
                for part in range(PIECES):
                    split_high(NBLK * g + BLK, 0, part)
                act.wait_ge(pv_done, UNITS * (g + 1))
                for pair in range(2):
                    o_high(0, 0, pair)
                unit_step(g, UNITS // 8, 2, UNITS + 2)
                act.wait_ge(o_stored, B * g + B)
                for q in range(OBLK):
                    if q:
                        act.wait_ge(d_done, 16 * g + 4 * q + D_AHEAD - 4)
                        for part in range(PIECES):
                            split_high(NBLK * g + BLK + q, q % 2, part)
                    for c in range(TC):
                        for pair in range(2):
                            if q or c:
                                act.wait_ge(d_done, 16 * g + 4 * q + 2 * c + pair + D_AHEAD - 1)
                                o_high(q, c, pair)

        @block.vector
        def _(dve):
            dve.sem_inc(d_done, D_AHEAD)
            dve.sem_inc(d_added, ADD_AHEAD)
            dve.sem_inc(w_lo_done, LO_AHEAD)
            dve.sem_inc(l1_added, L1_AHEAD)
            steps = [0]

            def link(ins):
                steps[0] += 1
                ins.then_inc(setup, 1)
                dve.wait_ge(setup, steps[0])

            def col(c):
                return consts[:, c:c + 1]

            dve.wait_ge(const_in, 48)
            nc.vector.tensor_scalar(mask0[:], ids0[:], col(C_P16), None, ALU.is_equal)
            nc.vector.tensor_scalar(mask2[:], ids2[:], col(C_P32), 0.5, ALU.is_equal, ALU.mult)
            nc.vector.tensor_scalar(mask24[:], ids2[:], 4.0, 0.5, ALU.is_equal,
                                    ALU.mult).then_inc(masks_ready, 1)
            dve.wait_ge(masks_ready, 1)

            def per_seq(ap, n=16):
                return ap.unsqueeze(2).to_broadcast([ap.shape[0], n, S])

            def seqs(ap):
                return ap.rearrange("p (b t) -> p b t", t=S)

            for c in range(TC):
                dve.wait_ge(l0_low_done, c + 1)
                nc.vector.tensor_tensor(seqs(low[:, chunk(c)]), seqs(ps[:, c]),
                                        per_seq(mask0[:, 16 * c:16 * c + 16]),
                                        ALU.mult).then_inc(l0_low_masked, 1)

            def add_to_x(bank, oc, c, done):
                nc.vector.tensor_tensor(x_t[:, oc, chunk(c)], x_t[:, oc, chunk(c)], ps[:, bank],
                                        ALU.add).then_inc(done, 1)

            for c in range(TC):
                for oc in range(KC):
                    dve.wait_ge(l0_done, KC * c + oc + 1)
                    add_to_x((2 + KC * c + oc) % 8, oc, c, l0_added)

            dve.wait_ge(setup_in, 16 * 14)
            nc.vector.tensor_scalar(pos[:], len_tok[:], col(C_M32), None, ALU.add).then_inc(setup, 1)
            steps[0] += 1
            nc.vector.tensor_copy(len_b[:, 0:B], lens[:])
            nc.vector.memset(len_b[:, B:B + 1], 0.0)
            nc.vector.tensor_copy(iota16[:], iota_f[:])
            nc.vector.tensor_scalar(v_rows[:, 0], bt_v[:], float(PSIZE), col(C_M32), ALU.mult, ALU.add)
            nc.vector.tensor_scalar(k_rows[:, 0], bt_k[:], float(P), col(C_P), ALU.mult, ALU.add)
            dve.wait_ge(setup, 1)
            link(nc.vector.tensor_tensor(
                ang[:], pos[:].unsqueeze(2).to_broadcast([P, TT, HD // 2]),
                consts[:, C_FREQ:C_N].unsqueeze(1).to_broadcast([P, TT, HD // 2]), ALU.mult))
            nc.vector.tensor_scalar(v_rows[:, 1], v_rows[:, 0], float(PAGES * PSIZE), None, ALU.add)
            nc.vector.tensor_scalar(k_rows[:, 1], k_rows[:, 0], float(PAGES * P), None, ALU.add)
            link(nc.vector.tensor_scalar(cyc[:], ang[:], 1.0 / TWO_PI, ROUND, ALU.mult, ALU.add))
            link(nc.vector.tensor_scalar(turns[:], cyc[:], ROUND, None, ALU.subtract))
            for part in (PI_A, PI_B, PI_C):
                link(nc.vector.scalar_tensor_tensor(ang[:], turns[:], -part, ang[:], ALU.mult, ALU.add))
            nc.vector.tensor_scalar(ang[:], ang[:], PI_IN, -PI_IN, ALU.min, ALU.max).then_inc(rad_ready, 1)

            def add_l1(b, s, par):
                cols = x_t[:, :, ds(S * b, S)]
                own = ps[:, 4 - 4 * par + s].rearrange("p (k t) -> p k t", k=KC)[:, :, S * s:S * (s + 1)]
                nc.vector.tensor_tensor(cols, cols, own, ALU.add).then_inc(l1_added, 1)

            def layer2(c):
                dve.wait_ge(l2_low_done, 2 * c + 1)
                nc.vector.tensor_tensor(seqs(low[:, chunk(c)]), seqs(ps[:, 4]),
                                        per_seq(mask2[:, 16 * c:16 * c + 16]), ALU.mult)
                dve.wait_ge(l2_low_done, 2 * c + 2)
                nc.vector.tensor_tensor(seqs(low4[:, chunk(c)]), seqs(ps[0:R2, 5]),
                                        per_seq(mask24[0:R2, 16 * c:16 * c + 16]),
                                        ALU.mult).then_inc(l2_low4_masked, 1)
                dve.wait_ge(l2_low4_masked, c + 1)
                nc.vector.tensor_tensor(low[0:R2, chunk(c)], low[0:R2, chunk(c)], low4[:, chunk(c)],
                                        ALU.add).then_inc(l2_low_masked, 1)
                dve.wait_ge(l2_done, c + 1)
                for oc in range(KC):
                    add_to_x(oc, oc, c, l2_added)
                if c:
                    for kc in range(KC):
                        dve.wait_ge(l2_added, KC * c + kc + 1)
                        nc.vector.tensor_copy(x_hi[:, kc, chunk(c)], x_t[:, kc, chunk(c)]
                                              ).then_inc(x_hi_ready, 1)
                for kc in range(KC):
                    dve.wait_ge(x_hi_ready, KC * c + kc + 1)
                    nc.vector.tensor_tensor(x_lo[:, kc, chunk(c)], x_t[:, kc, chunk(c)],
                                            x_hi[:, kc, chunk(c)].bitcast(F32),
                                            ALU.subtract).then_inc(x_lo_ready, 1)

            def rope_tables():
                dve.wait_ge(sin_ready, 1)
                link(nc.vector.tensor_tensor(cos_t[:], sin_h[:], sin_h[:], ALU.mult))
                link(nc.vector.tensor_scalar(cos_t[:], cos_t[:], -2.0, 1.0, ALU.mult, ALU.add))
                half = HD // 2
                for n in range(2):
                    for h in range(2):
                        cols = slice(half * h, half * (h + 1))
                        w = norm_w[:, n, cols].unsqueeze(1).to_broadcast([P, TT, half])
                        nc.vector.tensor_tensor(rope_c[:, n, :, cols], cos_t[:], w, ALU.mult)
                        nc.vector.scalar_tensor_tensor(rope_s[:, n, :, cols], sin_t[:], 1.0 - 2.0 * h, w,
                                                       ALU.mult, ALU.mult)

            for c in range(TC):
                with dve.Fori(0, 2) as i:
                    for par in range(2):
                        dve.wait_ge(l1_done, 8 * i + (16 * c + 4 * par + 4))
                        for s in range(4):
                            add_l1(8 * i + (16 * c + 4 * par + s), s, par)
                if c == 0:
                    rope_tables()
                layer2(c)

            def heads(ap):
                return ap.rearrange("p (h d) -> p h d", h=4)

            def scale_tile(g, m, t, first):
                dve.wait_ge(summed, QKT * g + m + 1)
                dve.wait_ge(rstd_done, QKT * g + m + 1)
                if not (first and t < 2):
                    dve.wait_ge(qk_turned, QKT * g + m - 1)
                p = t % 2
                nc.vector.tensor_tensor(
                    heads(r_out[:, p]), heads(r_cos[:, p]),
                    stat[:, p, RSTD].unsqueeze(2).to_broadcast([P, 4, HD]), ALU.mult).then_inc(rn_done, 1)

            def newton_step(g, m, t):
                dve.wait_ge(y0_done, QKT * g + m + 1)
                y, v = stat[:, t % 2, Y0], stat[:, t % 2, VAR]
                w, r = stat[:, t % 2, NT], stat[:, t % 2, RSTD]
                nc.vector.tensor_tensor(w, y, y, ALU.mult).then_inc(newton, 1)
                dve.wait_ge(newton, 3 * (QKT * g + m) + 1)
                nc.vector.tensor_tensor(w, w, v, ALU.mult).then_inc(newton, 1)
                dve.wait_ge(newton, 3 * (QKT * g + m) + 2)
                nc.vector.tensor_scalar(w, w, -0.5, 1.5, ALU.mult, ALU.add).then_inc(newton, 1)
                dve.wait_ge(newton, 3 * (QKT * g + m) + 3)
                nc.vector.tensor_tensor(r, y, w, ALU.mult).then_inc(rstd_done, 1)

            def qk_tile(g, j, t, first, n):
                m = 8 * j + t
                p = t % 2
                dve.wait_ge(sq_done, QKT * g + m + 1)
                nc.vector.tensor_scalar(stat[:, p, VAR], stat[:, p, SQ], 1.0 / HD, EPS,
                                        ALU.mult, ALU.add).then_inc(var_done, 1)
                dve.wait_ge(var_done, QKT * g + m + 1)
                nc.vector.reciprocal(stat[:, p, INV], stat[:, p, VAR]).then_inc(inv_done, 1)
                if not (first and t < 2):
                    dve.wait_ge(rn_done, QKT * g + m - 1)
                for dst, tab in ((r_cos, rope_c), (r_sin, rope_s)):
                    ins = nc.vector.tensor_tensor(heads(dst[:, p]), heads(ps[:, t % 4]),
                                                  tab[:, n, t].unsqueeze(1).to_broadcast([P, 4, HD]), ALU.mult)
                ins.then_inc(roped, 1)
                if not (first and t == 0):
                    scale_tile(g, m - 1, (t - 1) % 8, first and t - 1 < 2)
                newton_step(g, m, t)

            def batch_mask(g, b, p, first):
                if not first:
                    dve.wait_ge(max_done, UNITS * g + 4 * b - 4)
                nc.vector.tensor_scalar(mask[:, p, 0:L], iota16[:], len_b[:, ds(b, 1)], NEG,
                                        ALU.is_ge, ALU.mult).then_inc(mask_done, 1)

            def unit_step(g, i, e, c):
                s = 8 * i + e
                p = c % 2
                if 2 <= c < UNITS + 2:
                    dve.wait_ge(exp_done, UNITS * g + s - 1)
                    if c >= 4:
                        dve.wait_ge(o_norm, UNITS * g + s - 3)
                    nc.vector.reciprocal(row_inv[:, p:p + 1], row_sum[:, p:p + 1]).then_inc(inv_l, 1)
                if c < UNITS:
                    b = 2 * i + e // 4
                    if e % 4 == 0:
                        dve.wait_ge(mask_done, (B + 1) * g + b + 1)
                    dve.wait_ge(s_done, UNITS * g + s + 1)
                    settle(dve)
                    nc.vector.tensor_tensor_reduce(
                        out=sm[:, p], in0=ps[:, 2 * p:2 * p + 2].rearrange("p b n -> p (b n)")[:, SC:SC + KEYS],
                        in1=mask[:, e // 4], scale=-SCALE, scalar=BIG, op0=ALU.add, op1=ALU.min,
                        accum_out=sm_min[:, p:p + 1]).then_inc(max_done, 1)
                    if e % 4 == 2:
                        batch_mask(g, b + 1, 1 - e // 4, c < 4)
                if 2 <= c < UNITS + 2:
                    dve.wait_ge(inv_l, UNITS * g + s - 1)
                    dve.wait_ge(pv_done, UNITS * g + s - 1)
                    if c >= 4:
                        dve.wait_ge(o_turned, UNITS * g + s - 3)
                    nc.vector.tensor_scalar(o_sb[:, p], ps[:, 6, 0:P], row_inv[:, p:p + 1], None,
                                            ALU.mult).then_inc(o_norm, 1)
                if 1 <= c <= UNITS:
                    dve.wait_ge(p_turned, UNITS * g + s)
                    if c >= 3:
                        dve.wait_ge(pv_done, UNITS * g + s - 2)
                    nc.vector.tensor_copy(pt[:, 1 - p, 0:PTA * P], ps[:, 4, 0:PTA * P]).then_inc(pt_a, 1)

            with dve.Fori(0, HALVES) as g:
                for t in range(TT):
                    qk_tile(g, 0, t, True, 0)
                with dve.Fori(0, 2) as i:
                    for e in range(2):
                        for t in range(TT):
                            qk_tile(g, 2 * i + (1 + e), t, False, 1)
                scale_tile(g, QKT - 1, 7, False)
                dve.wait_ge(proj_done, 48 * g + 48)
                settle(dve)
                nc.vector.memset(pr[:, :, KEYS:KPAD], 0.0)
                nc.vector.memset(mask[:, :, L:KEYS], 0.0)
                batch_mask(g, 0, 0, True)
                for c in range(8):
                    unit_step(g, 0, c, c)
                with dve.Fori(1, UNITS // 8) as i:
                    for e in range(8):
                        unit_step(g, i, e, 8 + e)
                for e in range(2):
                    unit_step(g, UNITS // 8, e, UNITS + e)
                with dve.Fori(0, 2) as i:
                    for e in range(2):
                        for c in range(TC):
                            for pair in range(2):
                                dve.wait_ge(o_hi_ready, 16 * g + 8 * i + 4 * e + 2 * c + pair + 1)
                                nc.vector.tensor_tensor(
                                    o_lo[:, pair].rearrange("p h (b t) -> p b h t", t=S),
                                    qk[:, 16 * c:16 * (c + 1), ds(8 * i + (KVH + 4 * e + 2 * pair), 2), :],
                                    o_hi[:, pair].bitcast(F32).rearrange("p h (b t) -> p b h t", t=S),
                                    ALU.subtract).then_inc(o_lo_ready, 1)
                for c in range(TC):
                    dve.wait_ge(d_done, 16 * g + 14 + 2 * c + D_AHEAD)
                    for oc in range(KC):
                        add_to_x(KC * c + oc, oc, c, d_added)

        @block.tensor
        def _(pe):
            def mm(o, lhsT, rhs, start, stop):
                return nc.tensor.matmul(o, lhsT, rhs, start=start, stop=stop)

            pe.wait_ge(w0b_in, 16)
            for c in range(TC):
                pe.wait_ge(x_in[c], 16)
                for kc in range(KC):
                    ins = mm(ps[:, c], w0b[:, kc], x_t[:, kc, chunk(c)], kc == 0, kc == KC - 1)
                ins.then_inc(l0_low_done, 1)
            pe.wait_ge(w0a_in, 16)
            for c in range(TC):
                pe.wait_ge(l0_low_masked, TC if c else 1)
                for oc in range(KC):
                    mm(ps[:, (2 + KC * c + oc) % 8], w0a[:, tile(oc)], low[:, chunk(c)], True,
                       True).then_inc(l0_done, 1)

            def expert(t, s, par):
                b = 4 * t + s
                pe.wait_ge(exp_in[s], 16 * t + 16)
                pe.wait_ge(l1_added, b + 1)
                for oc in range(KC):
                    for kc in range(KC):
                        ins = mm(ps[:, 4 - 4 * par + s, tile(oc)], w_exp[:, s, kc, tile(oc)],
                                 x_t[:, kc, ds(P * t, P)], kc == 0, kc == KC - 1)
                ins.then_inc(l1_done, 1)

            pe.wait_ge(l0_added, TC * KC)
            for c in range(TC):
                if c:
                    pe.wait_ge(l2_low_masked, c)
                    pe.wait_ge(l2_added, KC * c)
                with pe.Fori(0, 2) as i:
                    for par in range(2):
                        for s in range(4):
                            expert(2 * i + (4 * c + par), s, par)
                pe.wait_ge(l1_added, 16 * (c + 1) + L1_AHEAD)
                if c == 0:
                    pe.wait_ge(w2_in, 16 * 6)
                    pe.wait_ge(l0_added, TC * KC)
                else:
                    pe.wait_ge(l2_added, KC)
                for n, (cols, o) in enumerate(((slice(0, P), ps[:, 4]), (slice(P, N2 * R2), ps[0:R2, 5]))):
                    for kc in range(KC):
                        ins = mm(o, w2a[:, kc, cols], x_t[:, kc, chunk(c)], kc == 0, kc == KC - 1)
                    ins.then_inc(l2_low_done, 1)
                for oc in range(KC):
                    for kc in range(KC):
                        mm(ps[:, oc], w2[:, kc, tile(oc)], x_t[:, kc, chunk(c)], kc == 0, False)
                pe.wait_ge(l2_low_masked, c + 1)
                for oc in range(KC):
                    ins = mm(ps[:, oc], w2b[:, tile(oc)], low[:, chunk(c)], False, True)
                ins.then_inc(l2_done, 1)

            def project(t, par, n_w=None):
                for kc in range(KC):
                    if n_w is not None:
                        pe.wait_ge(w_lo_done, n_w + LO_AHEAD + PIECES // KC * (kc + 1))
                    for n, (x, w) in enumerate(((x_hi, w_hi), (x_hi, w_lo), (x_lo, w_hi))):
                        ins = mm(ps[:, t % 4], x[:, kc, tile(t)], w[par][:, chunk(kc)],
                                 kc == 0 and n == 0, kc == KC - 1 and n == 2)
                ins.then_inc(proj_done, 1)

            def turn_qk(g, m, t, first):
                pe.wait_ge(rn_done, QKT * g + m + 1)
                if not (first and t < 2):
                    pe.wait_ge(qk_stored, QKT * g + m - 1)
                for h in range(4):
                    ins = nc.tensor.transpose(ps[:, 4 + t % 2, tile(h)], r_out[:, t % 2, tile(h)], ident)
                ins.then_inc(qk_turned, 1)

            def block_of(g, j, par, first):
                if not first:
                    pe.wait_ge(w_lo_done, PIECES * (NBLK * g + j + 1) + LO_AHEAD)
                for t in range(TT):
                    m = 8 * j + t
                    if first and t % 4 == 0:
                        pe.wait_ge(x_lo_ready, KC * (t // 4 + 1))
                    if first and t < 4:
                        pe.wait_ge(l2_added, KC + t + 1)
                        pe.wait_ge(d_added, 8 * g + ADD_AHEAD - 7 + t)
                    else:
                        pe.wait_ge(roped, QKT * g + m - 3)
                    project(t, par, PIECES * NBLK * g if first and t == 0 else None)
                    if t >= TLAG:
                        turn_qk(g, m - TLAG, t - TLAG, first)
                    elif not first:
                        turn_qk(g, m - TLAG, t - TLAG + TT, False)

            def scores(g, s, c, e):
                p, b2, k = c % 2, e // 4, e % 4
                if k == 0:
                    pe.wait_ge(q_in[b2], 32 * nth[0] + 32)
                    pe.wait_ge(k_in[b2], 16 * SPP * nth[0] + 16 * SPP)
                    pe.wait_ge(k_in2[b2], 16 * PPP * nth[0] + 16 * PPP)
                if c < 2:
                    pe.wait_ge(v_copied, 8 * g + TT - 2 + 2 * c)
                else:
                    pe.wait_ge(max_done, UNITS * g + s - 1)
                q = qk_st[b2][:, REP * k:REP * (k + 1), :].rearrange("p h t -> p (h t)")
                mm(ps[:, 2 * p, SC:512], q, k_buf[b2][:, 0:KA, k], True, True)
                mm(ps[:, 2 * p + 1, 0:KEYS - KA * S], q, k_buf[b2][:, KA:NPP + 1, k], True,
                   True).then_inc(s_done, 1)

            def values(g, s, c, e):
                p, b2, k = c % 2, e // 4, e % 4
                pe.wait_ge(pt_a, UNITS * g + s + 1)
                pe.wait_ge(pt_b, UNITS * g + s + 1)
                if k == 0:
                    pe.wait_ge(v_in[b2], 16 * VCH * nth_v[0] + 16 * VCH)
                    pe.wait_ge(vn_in[b2], 16 * nth_v[0] + 16)
                if c >= 1:
                    pe.wait_ge(o_norm, UNITS * g + s)
                for ch in range(KCH):
                    ins = mm(ps[:, 6, 0:P], pt[:, p, tile(ch)], v_buf[b2][:, ch, HD * k:HD * (k + 1)],
                             ch == 0, ch == KCH - 1)
                ins.then_inc(pv_done, 1)

            def turn_o(g, s, c, e, b):
                pe.wait_ge(o_norm, UNITS * g + s + 1)
                if e % 4 == 0 and c >= 4:
                    pe.wait_ge(o_stored, B * g + b)
                nc.tensor.transpose(ps[:, 7, tile(e % 4)], o_sb[:, c % 2], ident).then_inc(o_turned, 1)

            def turn_p(g, s, c):
                pe.wait_ge(exp_done, UNITS * g + s + 1)
                if c >= 1:
                    pe.wait_ge(pt_a, UNITS * g + s)
                    pe.wait_ge(pt_b, UNITS * g + s)
                for ch in range(KCH):
                    o = ps[:, 4, tile(ch)] if ch < PTA else ps[:, 5, tile(ch - PTA)]
                    ins = nc.tensor.transpose(o, pr[:, c % 2, tile(ch)], ident)
                ins.then_inc(p_turned, 1)

            nth, nth_v = [0], [0]

            def unit_step(g, i, e, c):
                s = 8 * i + e
                nth[0] = 16 * g + i
                nth_v[0] = 16 * g + i + (0 if e >= 2 else -1)
                if c < UNITS:
                    scores(g, s, c, e)
                if 2 <= c < UNITS + 2:
                    values(g, s - 2, c - 2, (e - 2) % 8)
                if 3 <= c:
                    turn_o(g, s - 3, c - 3, (e - 3) % 8, 2 * i + (e - 3) // 4)
                if 1 <= c <= UNITS:
                    turn_p(g, s - 1, c - 1)

            with pe.Fori(0, HALVES) as g:
                block_of(g, 0, 0, True)
                with pe.Fori(0, 2) as i:
                    for e in range(2):
                        block_of(g, 2 * i + (1 + e), 1 - e, False)
                pe.wait_ge(w_lo_done, PIECES * (NBLK * g + BLK) + LO_AHEAD)
                for t in range(TT):
                    if t < 4:
                        pe.wait_ge(roped, QKT * g + QKT + t - 3)
                    else:
                        pe.wait_ge(v_copied, 8 * g + t - 3)
                    project(t, 1)
                    if t < TLAG:
                        turn_qk(g, QKT - TLAG + t, TT - TLAG + t, False)
                for c in range(8):
                    unit_step(g, 0, c, c)
                with pe.Fori(1, UNITS // 8) as i:
                    for e in range(8):
                        unit_step(g, i, e, 8 + e)
                for e in range(3):
                    unit_step(g, UNITS // 8, e, UNITS + e)
                for q in range(OBLK):
                    par = q % 2
                    pe.wait_ge(w_lo_done, PIECES * (NBLK * g + BLK + q + 1) + LO_AHEAD)
                    for c in range(TC):
                        for pair in range(2):
                            pe.wait_ge(o_lo_ready, 16 * g + 4 * q + 2 * c + pair + 1)
                            for h in range(2):
                                for oc in range(KC):
                                    cols = slice(512 * (2 * pair + h) + P * oc, 512 * (2 * pair + h) + P * (oc + 1))
                                    for n, (w, o) in enumerate(((w_hi, o_hi), (w_hi, o_lo), (w_lo, o_hi))):
                                        ins = mm(ps[:, KC * c + oc], w[par][:, cols], o[:, pair, h],
                                                 q == 0 and pair == 0 and h == 0 and n == 0,
                                                 q == OBLK - 1 and pair == 1 and h == 1 and n == 2)
                            ins.then_inc(d_done, 1)


def kernel(x, itok_B_3_7, itok_B_0_15, itok_B_0_2, itok_Bx16_0_63, itok_B_207_1644,
           L0_cond_A, L0_cond_B, L1_cond_weight, L2_cond_W, L2_cond_lora_A, L2_cond_lora_B_w,
           L3_cond_Wq, L3_cond_Wk, L3_cond_Wv, L3_cond_Wo, L3_cond_q_norm_w, L3_cond_k_norm_w,
           L3_cond_k_cache, L3_cond_v_cache):
    import numpy as np
    import concourse.bacc as bacc
    from concourse.bass_utils import run_bass_kernel_spmd

    def fold(w):
        w = np.asarray(w)
        return w.reshape(w.shape[0], KC, P).transpose(2, 1, 0)

    def blocks(w, g, n):
        w = np.asarray(w)[g * n * 512:(g + 1) * n * 512]
        return [fold(w[512 * j:512 * (j + 1)]).reshape(P, BW) for j in range(n)]

    wo = np.asarray(L3_cond_Wo).reshape(DM, HALVES, OBLK, 4, HD).transpose(1, 2, 4, 3, 0)
    l3_w = []
    for g in range(HALVES):
        l3_w += blocks(L3_cond_Wk, g, 1) + blocks(L3_cond_Wq, g, OBLK) + blocks(L3_cond_Wv, g, 1)
        l3_w += [wo[g, j].reshape(P, BW) for j in range(OBLK)]
    kc = np.asarray(L3_cond_k_cache).reshape(PAGES, PSIZE, HALVES, KVH, HD).transpose(2, 0, 4, 3, 1)
    kc = np.ascontiguousarray(kc)
    vc = np.asarray(L3_cond_v_cache).reshape(PAGES, PSIZE, HALVES, KVH * HD).transpose(2, 0, 1, 3)
    const = np.zeros((P, C_N), np.float32)
    rows = np.arange(P)
    const[:, C_ID:C_ID + P] = np.eye(P)
    const[:, C_P16], const[:, C_P32], const[:, C_M32], const[:, C_P] = rows // R0, rows // R2, rows % S, rows
    const[:, C_FREQ:] = 1.0 / 10000.0 ** (np.arange(0, HD, 2) / HD)
    lora_a = np.asarray(L2_cond_lora_A)
    lens, pages = np.asarray(itok_B_207_1644), np.asarray(itok_Bx16_0_63)
    arrays = {
        "lens_q": lens.reshape(TT, BPT).T, "pages_q": pages.reshape(B, VCH, P // PSIZE).transpose(2, 0, 1),
        "pages_k": pages[:, SPP:],
        "x_t": fold(np.asarray(x).reshape(T, DM)),
        "ids0": itok_B_3_7, "ids1": itok_B_0_15, "ids2": itok_B_0_2,
        "pages": pages, "lens": lens,
        "l0_b": fold(np.asarray(L0_cond_B).reshape(N0 * R0, DM)),
        "l0_a": np.asarray(L0_cond_A).transpose(0, 2, 1).reshape(N0 * R0, DM),
        "l1_w": np.asarray(L1_cond_weight).reshape(16, DM, KC, P).transpose(0, 3, 2, 1),
        "l2_w": fold(L2_cond_W),
        "l2_a": fold(lora_a.transpose(0, 2, 1).reshape(N2 * R2, DM)),
        "l2_b": np.asarray(L2_cond_lora_B_w).T,
        "l3_w": np.stack(l3_w),
        "k_norm": L3_cond_k_norm_w, "q_norm": L3_cond_q_norm_w,
        "k_t": kc.reshape(HALVES * PAGES, HD, KVH, PSIZE),
        "k_rows": kc.reshape(HALVES * PAGES * HD, KVH * PSIZE),
        "v_rows": vc.reshape(HALVES * PAGES * PSIZE, KVH * HD),
        "consts": const, "iota": np.arange(L, dtype=np.float32),
    }
    arrays = {f"in_{n}": np.ascontiguousarray(v) for n, v in arrays.items()}
    nc = bacc.Bacc("TRN2", target_bir_lowering=False, num_devices=1)
    a = {n[3:]: nc.dram_tensor(n, v.shape, mybir.dt.from_np(v.dtype), kind="ExternalInput").ap()
         for n, v in arrays.items()}
    a["v_new"] = nc.dram_tensor("v_new_dram", [HALVES * B, S, KVH * HD], F32, kind="Internal").ap()
    out = nc.dram_tensor("out_t", [P, KC, T], F32, kind="ExternalOutput").ap()
    build(nc, a, out)
    r = run_bass_kernel_spmd(nc, [arrays], core_ids=[0])
    got = np.asarray(r.results[0]["out_t"])
    return np.ascontiguousarray(got.transpose(2, 1, 0).reshape(B, S, DM))
```

```python
from contextlib import ExitStack

import concourse.bass as bass
from concourse import mybir

F32 = mybir.dt.float32
F32R = mybir.dt.float32r
BF16 = mybir.dt.bfloat16
F16 = mybir.dt.float16
I32 = mybir.dt.int32
I16 = mybir.dt.int16
ALU = mybir.AluOpType
ACT = mybir.ActivationFunctionType
ds = bass.ds

P = 128
B, S, DM = 32, 32, 512
T = B * S
KC = DM // P
TC = T // 512
TT = T // P
BPT = P // S
BPC = 512 // S
HD = 128
HQ, HK = 32, 8
REP = HQ // HK
HALVES = 2
KVH = HK // HALVES
QH = HQ // HALVES
PAGES, PSIZE, NPP = 64, 32, 16
L = NPP * PSIZE
KEYS = L + S
KPAD = 640
KCH = KPAD // P
VCH = L // P
SLOTS = KVH + QH
BLK = 6
OBLK = 4
NBLK = BLK + OBLK
BW = KC * 512
QKT = 5 * TT
PROJ = BLK * TT
UNITS = B * KVH
SPP = 13
PPP = NPP - SPP
PIECES = 8
PW = BW // PIECES
TLAG = 3
PTA = 2
R0, N0 = 16, 8
R2, N2 = 32, 5
EPS = 1e-6
SCALE = HD ** -0.5
NEG = -1e30
BIG = 3e38
TWO_PI = 6.283185307179586
ROUND = 1.5 * 2.0 ** 23
PI_A = 6.28125
PI_B = 0.0019350051879882812
PI_C = TWO_PI - PI_A - PI_B
PI_IN = 3.1415925
C_ID, C_P16, C_P32, C_M32, C_P, C_FREQ = 0, 128, 129, 130, 131, 132
C_N = C_FREQ + HD // 2


def build(nc, a, out):
    with ExitStack() as ctx:
        def sb(name, shape, dt=F32):
            return ctx.enter_context(nc.sbuf_tensor(name, shape, dt))

        def sem(name):
            return ctx.enter_context(nc.semaphore(name))

        x_t = sb("x_t", [P, KC, T])
        rope_c = sb("rope_c", [P, 2, TT, HD])
        rope_s = sb("rope_s", [P, 2, TT, HD])
        consts = sb("consts_sb", [P, C_N])
        ident = consts[:, C_ID:C_ID + P]
        iota16 = sb("iota16", [P, L], F16)
        len_b = sb("len_b", [P, B + 1])
        v_rows = sb("v_rows", [P, HALVES, B, VCH], I16)
        k_rows = sb("k_rows", [P, HALVES, B, PPP], I16)
        v_idx = sb("v_idx", [P, 2, VCH], I32)
        k_idx = sb("k_idx", [P, 2, PPP], I32)
        ids_row = sb("ids_row", [1, B], I32)
        pages_row = sb("pages_row", [1, B, NPP], I32)
        stat = sb("stat", [P, 2, 6, 4])
        SQ, VAR, INV, Y0, NT, RSTD = range(6)
        sm_min = sb("sm_min", [P, 2])
        row_sum = sb("row_sum", [P, 2])
        warm = sb("warm", [P, 1])
        row_inv = sb("row_inv", [P, 2])
        at = [-(-nc.sbuf_base // 32) * 32]

        def place(name, shape, dt=F32, p=P):
            t = nc.alloc_sbuf_tensor_at(name, [p] + shape, dt, offset=at[0])
            size = mybir.dt.size(dt)
            for n in shape:
                size *= n
            at[0] += -(-size // 32) * 32
            return t

        split_at = at[0]
        x_hi = place("x_hi", [KC, T], F32R)
        x_lo = place("x_lo", [KC, T], F32R)
        split_end = at[0]
        at[0] = split_at
        k_hi = place("k_hi", [NPP + 1, KVH, S], F32R)
        k_lo = place("k_lo", [NPP + 1, KVH, S], F32R)
        q_hi = [place(f"q_hi{p}", [QH, S], F32R) for p in range(2)]
        q_lo = [place(f"q_lo{p}", [QH, S], F32R) for p in range(2)]
        assert at[0] <= split_end
        at[0] = split_end
        store_at = at[0]
        qk = place("qk", [B, SLOTS, S])
        region = at[0]
        at[0] = store_at
        ids0 = place("ids0", [B], I32)
        ids2 = place("ids2", [B], I32)
        mask0 = place("mask0", [B])
        mask2 = place("mask2", [B])
        mask24 = place("mask24", [B])
        lens = place("lens", [B], I32)
        len_tok = place("len_tok", [TT], I32)
        pos = place("pos", [TT])
        bt_v = place("bt_v", [B, VCH], I32)
        bt_k = place("bt_k", [B, PPP], I32)
        norm_w = place("norm_w", [2, HD])
        iota_f = place("iota_f", [L])
        ang = place("ang", [TT, HD // 2])
        cyc = place("cyc", [TT, HD // 2])
        turns = place("turns", [TT, HD // 2])
        sin_t = place("sin_t", [TT, HD // 2])
        sin_h = place("sin_h", [TT, HD // 2])
        cos_t = place("cos_t", [TT, HD // 2])
        at[0] = region
        w_exp = place("w_exp", [4, KC, DM])
        w0b = place("w0b", [KC, P])
        w0a = place("w0a", [DM])
        w2 = place("w2", [KC, DM])
        w2a = place("w2a", [KC, N2 * R2])
        w2b = place("w2b", [DM])
        low = place("low", [T])
        low4 = place("low4", [T], p=R2)
        at[0] = region
        w_in = place("w_in", [BW])
        w_hi0, w_lo0 = place("w_hi0", [BW], F32R), place("w_lo0", [BW], F32R)
        w_hi1, w_lo1 = place("w_hi1", [BW], F32R), place("w_lo1", [BW], F32R)
        w_hi, w_lo = (w_hi0, w_hi1), (w_lo0, w_lo1)
        work = at[0]
        r_sin = place("r_sin", [2, 512])
        r_cos = place("r_cos", [2, 512])
        r_out = place("r_out", [2, 512])
        b_sq = place("b_sq", [512])
        at[0] = work
        v_out = place("v_out", [TT, 512])
        at[0] = work
        o_hi = place("o_hi", [2, 2, 512], F32R)
        o_lo = place("o_lo", [2, 2, 512], F32R)
        at[0] = region
        k_buf, v_buf = [None] * 2, [None] * 2
        for p in range(2):
            k_buf[p] = place(f"k_buf{p}", [NPP + 1, KVH, S])
            v_buf[p] = place(f"v_buf{p}", [KCH, KVH * HD])
            if p == 0:
                early = PIECES - 2
                assert at[0] <= region + 4 * (2 * BW + early * PW)
                at[0] = region + 4 * (2 * BW + early * PW)
                sm = place("sm", [2, KEYS])
                pr = place("pr", [2, KPAD])
                pt = place("pt", [2, KPAD])
                o_sb = place("o_sb", [2, P])
                mask = place("mask", [2, KEYS], BF16)
                assert at[0] <= work
                at[0] = work
        KA = NPP // 2 + 1
        SC = 512 - KA * S

        ps = ctx.enter_context(nc.psum_tensor("ps", [P, 8, 512], F32))

        ids_in, const_in, setup_in = sem("ids_in"), sem("const_in"), sem("setup_in")
        x_in = [sem(f"x_in{n}") for n in range(3)]
        w0b_in, w0a_in, w2_in = sem("w0b_in"), sem("w0a_in"), sem("w2_in")
        exp_in = [sem(f"exp_in{s}") for s in range(4)]
        w_in_done = sem("w_in_done")
        kn_in = [sem(f"kn_in{p}") for p in range(2)]
        k_in = [sem(f"k_in{p}") for p in range(2)]
        k_rest_in = [sem(f"k_rest_in{p}") for p in range(2)]
        v_in = [sem(f"v_in{p}") for p in range(2)]
        vn_in = [sem(f"vn_in{p}") for p in range(2)]
        v_stored = [sem(f"v_stored{p}") for p in range(2)]
        out_stored = sem("out_stored")
        settled = sem("settled")
        setup = sem("setup")
        masks_ready = sem("masks_ready")
        rad_ready, sin_ready = sem("rad_ready"), sem("sin_ready")
        l0_low_done, l0_low_masked, l0_done, l0_added = (
            sem("l0_low_done"), sem("l0_low_masked"), sem("l0_done"), sem("l0_added"))
        l1_done, l1_added = sem("l1_done"), sem("l1_added")
        l2_low_done, l2_low4_masked, l2_low_masked, l2_done, l2_added = (
            sem("l2_low_done"), sem("l2_low4_masked"), sem("l2_low_masked"), sem("l2_done"), sem("l2_added"))
        x_hi_ready, x_lo_ready = sem("x_hi_ready"), sem("x_lo_ready")
        w_hi_done, w_lo_done = sem("w_hi_done"), sem("w_lo_done")
        proj_done, sq_done, var_done, inv_done, y0_done = (
            sem("proj_done"), sem("sq_done"), sem("var_done"), sem("inv_done"), sem("y0_done"))
        newton, rstd_done, roped, summed, rn_done = (
            sem("newton"), sem("rstd_done"), sem("roped"), sem("summed"), sem("rn_done"))
        qk_turned, qk_stored, v_copied = sem("qk_turned"), sem("qk_stored"), sem("v_copied")
        q_hi_done, k_hi_done, k_lo_done = sem("q_hi_done"), sem("k_hi_done"), sem("k_lo_done")
        v_padded, idx_copied, mask_done = sem("v_padded"), sem("idx_copied"), sem("mask_done")
        s_done, max_done, exp_done, p_turned = (
            sem("s_done"), sem("max_done"), sem("exp_done"), sem("p_turned"))
        pt_a, pt_b, pv_done, inv_l, o_norm, o_turned, o_stored = (
            sem("pt_a"), sem("pt_b"), sem("pv_done"), sem("inv_l"), sem("o_norm"),
            sem("o_turned"), sem("o_stored"))
        o_hi_ready, o_lo_ready, d_done, d_added = (
            sem("o_hi_ready"), sem("o_lo_ready"), sem("d_done"), sem("d_added"))
        L1_AHEAD = 8
        D_AHEAD, ADD_AHEAD, LO_AHEAD = 8, 8, PIECES

        block = ctx.enter_context(nc.Block())

        def chunk(c):
            return slice(512 * c, 512 * (c + 1))

        def piece(q):
            return slice(PW * q, PW * (q + 1))

        def pieces_at(t):
            first, last = round(PIECES * max(t - 1, 0) / 6), round(PIECES * min(t, 6) / 6)
            return range(first, last)

        def tile(t):
            return slice(P * t, P * (t + 1))

        def b_done(eng, g):
            for p in range(2):
                eng.wait_ge(v_stored[p], 4 * TT * g + 4 * TT)

        def settle(eng):
            eng.sem_inc(settled, 1)

        @block.sync
        def _(sp):
            sp.dma_start(ids_row[:], a["ids1"].unsqueeze(0)).then_inc(ids_in, 16)
            sp.dma_start(w0b[:], a["l0_b"]).then_inc(w0b_in, 16)
            for h in range(2):
                kcs = slice(KC // 2 * h, KC // 2 * (h + 1))
                sp.dma_start(x_t[:, kcs, chunk(0)], a["x_t"][:, kcs, chunk(0)]).then_inc(x_in[h], 16)
            sp.dma_start(w0a[:], a["l0_a"]).then_inc(w0a_in, 16)
            sp.dma_start(x_t[:, :, chunk(1)], a["x_t"][:, :, chunk(1)]).then_inc(x_in[2], 16)
            sp.wait_ge(ids_in, 16)

            def load_expert(b, s):
                e = sp.value_load(ids_row[0:1, ds(b, 1)], min_val=0, max_val=15)
                if not isinstance(b, int):
                    sp.wait_ge(l1_done, b - 3)
                sp.dma_start(w_exp[:, s], a["l1_w"][ds(e, 1)].rearrange("e p k n -> p (e k) n")
                             ).then_inc(exp_in[s], 16)

            for s in range(4):
                load_expert(s, s)
            sp.dma_start(w2[:], a["l2_w"]).then_inc(w2_in, 16)
            sp.dma_start(w2a[:], a["l2_a"]).then_inc(w2_in, 16)
            for r in range(P // R2):
                sp.dma_start(w2b[R2 * r:R2 * (r + 1)], a["l2_b"]).then_inc(w2_in, 16)
            with sp.Fori(1, B // 4) as i:
                for s in range(4):
                    load_expert(4 * i + s, s)
            sp.wait_ge(l1_done, B)

            def load_block(n):
                sp.wait_ge(w_lo_done, PIECES * n + LO_AHEAD)
                sp.dma_start(w_in[:], a["l3_w"][ds(n, 1)].rearrange("n p w -> p (n w)")
                             ).then_inc(w_in_done, 16)

            def load_cached(g, b, p, free=None):
                settle(sp)
                pages = nc.values_load_multi_w_load_instructions(
                    pages_row[0:1, ds(b, 1), 0:SPP], engines=[mybir.EngineType.SP], min_val=0,
                    max_val=PAGES - 1, skip_runtime_bounds_check_because="ids of cache pages")[1]
                if free is not None:
                    sp.wait_ge(k_lo_done, free)
                for j in range(SPP):
                    sp.dma_start(
                        k_buf[p][:, j],
                        a["k_t"][ds(PAGES * g + pages[j], 1)].rearrange("n p h t -> p (n h) t")
                    ).then_inc(k_in[p], 16)

            def load_new(b, p):
                sp.dma_start(k_buf[p][:, NPP], qk[:, ds(b, 1), 0:KVH].rearrange("p b h t -> p (b h) t")
                             ).then_inc(kn_in[p], 16)

            def load_values(g, b, p):
                sp.wait_ge(pv_done, UNITS * g + 4 * b - 4)
                settle(sp)
                sp.dma_start(v_buf[p][0:S, VCH], a["v_new"][ds(B * g + b, 1)].rearrange("n t w -> (n t) w")
                             ).then_inc(vn_in[p], 16)

            with sp.Fori(0, HALVES) as g:
                with sp.Fori(0, BLK) as j:
                    load_block(NBLK * g + j)

                def store_v(t):
                    sp.wait_ge(v_copied, 8 * g + (t + 2))
                    settle(sp)
                    sp.dma_start(
                        a["v_new"][ds(B * g + BPT * t, 2 * BPT)].rearrange("(u n) t w -> (n t) u w", u=2),
                        v_out[:, t:t + 2]).then_inc(v_stored[t // (TT // 2)], 16)

                sp.wait_ge(proj_done, PROJ * g + QKT)
                sp.wait_ge(w_lo_done, PIECES * (NBLK * g + BLK) + LO_AHEAD)
                load_cached(g, 0, 0)
                sp.wait_ge(qk_stored, QKT * g + QKT)
                settle(sp)
                load_new(0, 0)
                store_v(0)
                sp.wait_ge(v_padded, 2 * g + 2)
                for p in range(2):
                    sp.dma_start(v_buf[p][0:S, VCH], v_out[S * p:S * (p + 1), 0]).then_inc(vn_in[p], 16)
                store_v(2)
                sp.wait_ge(v_stored[0], 4 * TT * g + 4 * TT)
                for p in range(2):
                    sp.wait_ge(vn_in[p], 16 * (B // 2) * g + 16)
                load_cached(g, 1, 1)
                for t in range(TT // 2, TT, 2):
                    store_v(t)
                b_done(sp, g)
                load_new(1, 1)
                with sp.Fori(1, B // 2) as i:
                    for p in range(2):
                        b = 2 * i + p
                        load_cached(g, b, p, free=UNITS * g + 4 * b - 4)
                        load_new(b, p)
                        load_values(g, b, p)
                sp.wait_ge(k_lo_done, UNITS * (g + 1) - KVH)
                settle(sp)
                with sp.Fori(BLK, NBLK) as j:
                    load_block(NBLK * g + j)
            for c in range(TC):
                for oc in range(KC):
                    sp.wait_ge(d_added, ADD_AHEAD + 8 * (HALVES - 1) + KC * c + oc + 1)
                    sp.dma_start(out[:, oc, chunk(c)], x_t[:, oc, chunk(c)]).then_inc(out_stored, 16)
            sp.wait_ge(out_stored, 16 * TC * KC)

        @block.gpsimd
        def _(pool):
            def split_low(j, part):
                n, par = j
                cols = piece(part)
                pool.wait_ge(w_hi_done, PIECES * n + (part + 1))
                nc.gpsimd.tensor_tensor(w_lo[par][:, cols], w_in[:, cols],
                                        w_hi[par][:, cols].bitcast(F32),
                                        ALU.subtract).then_inc(w_lo_done, 1)

            def qk_tile(g, j, t, first, par):
                m = 8 * j + t
                for part in pieces_at(t):
                    split_low((NBLK * g + j + 1, 1 - par), part)
                pool.wait_ge(roped, QKT * g + m + 1)
                c4 = r_cos[:, t % 2].rearrange("p (h d) -> p h d", h=4)
                s4 = r_sin[:, t % 2].rearrange("p (h d) -> p h d", h=4)
                half = HD // 2
                nc.gpsimd.tensor_tensor(c4[:, :, 0:half], c4[:, :, 0:half], s4[:, :, half:HD], ALU.add)
                nc.gpsimd.tensor_tensor(c4[:, :, half:HD], c4[:, :, half:HD], s4[:, :, 0:half],
                                        ALU.add).then_inc(summed, 1)

            def fetch(g, b, p, first):
                if not first:
                    pool.wait_ge(k_lo_done, UNITS * g + 4 * b - 4)
                n = B * g + b
                row = k_rows[:, :].rearrange("p g b c -> p (g b) c")
                nc.gpsimd.tensor_copy(k_idx[:, p], row[:, ds(n, 1)]).then_inc(idx_copied, 1)
                pool.wait_ge(idx_copied, 2 * n + 1)
                settle(pool)
                for j in range(PPP):
                    pool.indirect_dma_start(
                        k_buf[p][:, SPP + j].rearrange("p h t -> p (h t)"), None, a["k_rows"],
                        bass.IndirectOffsetOnAxis(k_idx[:, p, j:j + 1], 0)).then_inc(k_rest_in[p], 16)
                if not first:
                    pool.wait_ge(pv_done, UNITS * g + 4 * b - 4)
                elif p == 1:
                    b_done(pool, g)
                    settle(pool)
                row = v_rows[:, :].rearrange("p g b c -> p (g b) c")
                nc.gpsimd.tensor_copy(v_idx[:, p], row[:, ds(n, 1)]).then_inc(idx_copied, 1)
                pool.wait_ge(idx_copied, 2 * n + 2)
                settle(pool)
                for c in range(VCH):
                    pool.indirect_dma_start(
                        v_buf[p][:, c], None, a["v_rows"],
                        bass.IndirectOffsetOnAxis(v_idx[:, p, c:c + 1], 0)).then_inc(v_in[p], 16)

            with pool.Fori(0, HALVES) as g:
                for part in range(PIECES):
                    split_low((NBLK * g, 0), part)
                for t in range(TT):
                    qk_tile(g, 0, t, True, 0)
                with pool.Fori(0, 2) as i:
                    for e in range(2):
                        for t in range(TT):
                            qk_tile(g, 2 * i + (1 + e), t, False, 1 - e)
                pool.wait_ge(proj_done, PROJ * g + QKT)
                settle(pool)
                for p in range(2):
                    nc.gpsimd.memset(v_buf[p][:, VCH], 0.0).then_inc(v_padded, 1)
                fetch(g, 0, 0, True)
                pool.wait_ge(v_stored[0], 4 * TT * g + 4 * TT)
                settle(pool)
                fetch(g, 1, 1, True)
                with pool.Fori(1, B // 2) as i:
                    for p in range(2):
                        fetch(g, 2 * i + p, p, False)
                for q in range(OBLK):
                    if q == 0:
                        pool.wait_ge(pv_done, UNITS * (g + 1) - KVH)
                    for part in range(PIECES):
                        if q == 0 and part == early:
                            pool.wait_ge(exp_done, UNITS * (g + 1) - 1)
                        split_low((NBLK * g + BLK + q, q % 2), part)

        @block.scalar
        def _(act):
            act.dma_start(consts[:], a["consts"]).then_inc(const_in, 16)
            act.dma_start(ids0[:], a["ids0"].partition_broadcast(P)).then_inc(const_in, 16)
            act.dma_start(ids2[:], a["ids2"].partition_broadcast(P)).then_inc(const_in, 16)
            act.dma_start(lens[:], a["lens"].partition_broadcast(P)).then_inc(setup_in, 16)
            for q in range(4):
                rows = slice(32 * q, 32 * (q + 1))
                act.dma_start(len_tok[rows], a["lens_q"][q].partition_broadcast(S)).then_inc(setup_in, 16)
                act.dma_start(bt_v[rows], a["pages_q"][q].partition_broadcast(PSIZE)).then_inc(setup_in, 16)
            act.dma_start(bt_k[:], a["pages_k"].partition_broadcast(P)).then_inc(setup_in, 16)
            act.dma_start(norm_w[:, 0], a["k_norm"].partition_broadcast(P)).then_inc(setup_in, 16)
            act.dma_start(norm_w[:, 1], a["q_norm"].partition_broadcast(P)).then_inc(setup_in, 16)
            act.dma_start(iota_f[:], a["iota"].partition_broadcast(P)).then_inc(setup_in, 16)
            act.dma_start(pages_row[:], a["pages"].unsqueeze(0)).then_inc(setup_in, 16)
            act.wait_ge(rad_ready, 1)
            nc.scalar.activation(sin_t[:], ang[:], ACT.Sin)
            nc.scalar.activation(sin_h[:], ang[:], ACT.Sin, scale=0.5).then_inc(sin_ready, 1)
            for kc in range(KC):
                act.wait_ge(l2_added, kc + 1)
                nc.scalar.copy(x_hi[:, kc, chunk(0)], x_t[:, kc, chunk(0)]).then_inc(x_hi_ready, 1)

            def split_high(n, par, part):
                cols = piece(part)
                if part == 0:
                    act.wait_ge(w_in_done, 16 * n + 16)
                nc.scalar.copy(w_hi[par][:, cols], w_in[:, cols]).then_inc(w_hi_done, 1)

            def store_qk(g, m, j, t):
                act.wait_ge(qk_turned, QKT * g + m + 1)
                nc.scalar.copy(
                    qk[:, BPT * t:BPT * (t + 1), ds(4 * j, 4), :],
                    ps[:, 4 + t % 2].rearrange("p (h b s) -> p b h s", h=4, b=BPT)
                ).then_inc(qk_stored, 1)

            def qk_tile(g, j, t, first, par):
                m = 8 * j + t
                for part in pieces_at(t):
                    split_high(NBLK * g + j + 1, 1 - par, part)
                act.wait_ge(proj_done, PROJ * g + m + 1)
                if not (first and t == 0):
                    act.wait_ge(sq_done, QKT * g + m)
                for h in range(4):
                    ins = nc.scalar.activation(b_sq[:, tile(h)], ps[:, t % 4, tile(h)], ACT.Square,
                                               accum_out=stat[:, t % 2, SQ, h:h + 1])
                ins.then_inc(sq_done, 1)
                act.wait_ge(inv_done, QKT * g + m + 1)
                if not (first and t < 2):
                    act.wait_ge(rstd_done, QKT * g + m - 1)
                nc.scalar.activation(stat[:, t % 2, Y0], stat[:, t % 2, INV], ACT.Sqrt).then_inc(y0_done, 1)
                if t >= TLAG:
                    store_qk(g, m - TLAG, j, t - TLAG)
                elif not first:
                    store_qk(g, m - TLAG, j - 1, t - TLAG + TT)

            def split_k(g, i, e):
                b2, k = e // 4, e % 4
                if k == 0:
                    n = 16 * g + i
                    act.wait_ge(k_in[b2], 16 * SPP * n + 16 * SPP)
                    act.wait_ge(k_rest_in[b2], 16 * PPP * n + 16 * PPP)
                    act.wait_ge(kn_in[b2], 16 * n + 16)
                nc.scalar.copy(k_hi[:, :, k], k_buf[b2][:, :, k]).then_inc(k_hi_done, 1)

            def split_q(b, b2, half):
                n = QH // 2
                nc.scalar.copy(q_hi[b2][:, n * half:n * (half + 1)], qk[
                    :, ds(b, 1), KVH + n * half:KVH + n * (half + 1), :].rearrange("p b h t -> p (b h) t")
                ).then_inc(q_hi_done, 1)

            def exp_unit(g, s, c):
                act.wait_ge(max_done, UNITS * g + s + 1)
                if c >= 2:
                    act.wait_ge(p_turned, UNITS * g + s - 1)
                nc.scalar.activation(pr[:, c % 2, 0:KEYS], sm[:, c % 2], ACT.Exp,
                                     bias=sm_min[:, c % 2:c % 2 + 1], scale=-1.0,
                                     accum_out=row_sum[:, c % 2:c % 2 + 1]).then_inc(exp_done, 1)

            def copy_pt(g, s, c):
                act.wait_ge(p_turned, UNITS * g + s + 1)
                if c >= 2:
                    act.wait_ge(pv_done, UNITS * g + s - 1)
                nc.scalar.copy(pt[:, c % 2, PTA * P:KPAD], ps[:, 5, 0:KPAD - PTA * P]).then_inc(pt_b, 1)

            def store_o(g, b, s):
                act.wait_ge(o_turned, UNITS * g + s + 1)
                nc.scalar.copy(qk[:, ds(b, 1), KVH:SLOTS, :].rearrange("p b h t -> p (b h t)"),
                               ps[:, 7, :]).then_inc(o_stored, 1)

            def unit_step(g, i, e, c):
                s = 8 * i + e
                if c >= 7 and c % 4 == 3:
                    store_o(g, 2 * i + (e // 4 - 1), s - 4)
                if c < UNITS - 2 and (e + 2) % 4:
                    split_k(g, i + (e + 2) // 8, (e + 2) % 8)
                if c < UNITS - 4 and e % 4 in (1, 2):
                    split_q(2 * i + (e // 4 + 1), 1 - e // 4, e % 4 - 1)
                if 1 <= c <= UNITS:
                    copy_pt(g, s - 1, c - 1)
                if c < UNITS:
                    exp_unit(g, s, c)
                if c < UNITS - 2 and (e + 2) % 4 == 0:
                    split_k(g, i + (e + 2) // 8, (e + 2) % 8)

            with act.Fori(0, HALVES) as g:
                act.wait_ge(d_done, 16 * g + D_AHEAD - 4)
                for part in range(PIECES):
                    split_high(NBLK * g, 0, part)
                for t in range(TT):
                    qk_tile(g, 0, t, True, 0)
                with act.Fori(0, 2) as i:
                    for e in range(2):
                        for t in range(TT):
                            qk_tile(g, 2 * i + (1 + e), t, False, 1 - e)
                nc.scalar.activation(warm[:], consts[:, C_P:C_P + 1], ACT.Exp, scale=0.0)
                for t in range(TT):
                    if t < TLAG:
                        store_qk(g, QKT - TLAG + t, 4, TT - TLAG + t)
                    if t < 2:
                        act.wait_ge(summed, QKT * g + QKT - 1 + t)
                    elif t < 4:
                        act.wait_ge(rn_done, QKT * g + QKT - 3 + t)
                    act.wait_ge(proj_done, PROJ * g + QKT + t + 1)
                    nc.scalar.copy(v_out[:, t], ps[:, t % 4]).then_inc(v_copied, 1)
                for e in range(2):
                    split_q(0, 0, e)
                    split_k(g, 0, e)
                for c in range(8):
                    unit_step(g, 0, c, c)
                with act.Fori(1, UNITS // 8 - 1) as i:
                    for e in range(8):
                        unit_step(g, i, e, 8 + e)
                for e in range(7):
                    unit_step(g, UNITS // 8 - 1, e, UNITS - 8 + e)
                act.wait_ge(pv_done, UNITS * (g + 1) - KVH)
                for part in range(PIECES):
                    if part == PIECES // 2:
                        unit_step(g, UNITS // 8 - 1, 7, UNITS - 1)
                    split_high(NBLK * g + BLK, 0, part)
                unit_step(g, UNITS // 8, 0, UNITS)

                def o_high(q, c, pair):
                    nc.scalar.copy(
                        o_hi[:, pair].rearrange("p h (b t) -> p b h t", t=S),
                        qk[:, 16 * c:16 * (c + 1), KVH + 4 * q + 2 * pair:KVH + 4 * q + 2 * pair + 2, :]
                    ).then_inc(o_hi_ready, 1)

                o_high(0, 0, 0)
                unit_step(g, UNITS // 8, 1, UNITS + 1)
                o_high(0, 0, 1)
                unit_step(g, UNITS // 8, 3, UNITS + 3)
                act.wait_ge(o_stored, B * g + B)
                for q in range(OBLK):
                    if q:
                        act.wait_ge(d_done, 16 * g + 4 * q + D_AHEAD - 4)
                        for part in range(PIECES):
                            split_high(NBLK * g + BLK + q, q % 2, part)
                    for c in range(TC):
                        for pair in range(2):
                            if q or c:
                                act.wait_ge(d_done, 16 * g + 4 * q + 2 * c + pair + D_AHEAD - 1)
                                o_high(q, c, pair)
                    if q == 1:
                        for c in range(TC):
                            for kc in range(KC):
                                nc.scalar.copy(x_hi[:, kc, chunk(c)], x_t[:, kc, chunk(c)]
                                               ).then_inc(x_hi_ready, 1)

        @block.vector
        def _(dve):
            dve.sem_inc(d_done, D_AHEAD)
            dve.sem_inc(d_added, ADD_AHEAD)
            dve.sem_inc(w_lo_done, LO_AHEAD)
            dve.sem_inc(l1_added, L1_AHEAD)
            steps = [0]

            def link(ins):
                steps[0] += 1
                ins.then_inc(setup, 1)
                dve.wait_ge(setup, steps[0])

            def col(c):
                return consts[:, c:c + 1]

            dve.wait_ge(const_in, 48)
            nc.vector.tensor_scalar(mask0[:], ids0[:], col(C_P16), None, ALU.is_equal)
            nc.vector.tensor_scalar(mask2[:], ids2[:], col(C_P32), 0.5, ALU.is_equal, ALU.mult)
            nc.vector.tensor_scalar(mask24[:], ids2[:], 4.0, 0.5, ALU.is_equal,
                                    ALU.mult).then_inc(masks_ready, 1)
            dve.wait_ge(masks_ready, 1)

            def per_seq(ap, n=16):
                return ap.unsqueeze(2).to_broadcast([ap.shape[0], n, S])

            def seqs(ap):
                return ap.rearrange("p (b t) -> p b t", t=S)

            for c in range(TC):
                dve.wait_ge(l0_low_done, c + 1)
                nc.vector.tensor_tensor(seqs(low[:, chunk(c)]), seqs(ps[:, c]),
                                        per_seq(mask0[:, 16 * c:16 * c + 16]),
                                        ALU.mult).then_inc(l0_low_masked, 1)

            def add_to_x(bank, oc, c, done):
                nc.vector.tensor_tensor(x_t[:, oc, chunk(c)], x_t[:, oc, chunk(c)], ps[:, bank],
                                        ALU.add).then_inc(done, 1)

            for c in range(TC):
                for oc in range(KC):
                    dve.wait_ge(l0_done, KC * c + oc + 1)
                    add_to_x((2 + KC * c + oc) % 8, oc, c, l0_added)

            dve.wait_ge(setup_in, 16 * 14)
            nc.vector.tensor_scalar(pos[:], len_tok[:], col(C_M32), None, ALU.add).then_inc(setup, 1)
            steps[0] += 1
            nc.vector.tensor_copy(len_b[:, 0:B], lens[:])
            nc.vector.memset(len_b[:, B:B + 1], 0.0)
            nc.vector.tensor_copy(iota16[:], iota_f[:])
            nc.vector.tensor_scalar(v_rows[:, 0], bt_v[:], float(PSIZE), col(C_M32), ALU.mult, ALU.add)
            nc.vector.tensor_scalar(k_rows[:, 0], bt_k[:], float(P), col(C_P), ALU.mult, ALU.add)
            dve.wait_ge(setup, 1)
            link(nc.vector.tensor_tensor(
                ang[:], pos[:].unsqueeze(2).to_broadcast([P, TT, HD // 2]),
                consts[:, C_FREQ:C_N].unsqueeze(1).to_broadcast([P, TT, HD // 2]), ALU.mult))
            nc.vector.tensor_scalar(v_rows[:, 1], v_rows[:, 0], float(PAGES * PSIZE), None, ALU.add)
            nc.vector.tensor_scalar(k_rows[:, 1], k_rows[:, 0], float(PAGES * P), None, ALU.add)
            link(nc.vector.tensor_scalar(cyc[:], ang[:], 1.0 / TWO_PI, ROUND, ALU.mult, ALU.add))
            link(nc.vector.tensor_scalar(turns[:], cyc[:], ROUND, None, ALU.subtract))
            for part in (PI_A, PI_B, PI_C):
                link(nc.vector.scalar_tensor_tensor(ang[:], turns[:], -part, ang[:], ALU.mult, ALU.add))
            nc.vector.tensor_scalar(ang[:], ang[:], PI_IN, -PI_IN, ALU.min, ALU.max).then_inc(rad_ready, 1)

            def add_l1(b, s, par):
                cols = x_t[:, :, ds(S * b, S)]
                own = ps[:, 4 - 4 * par + s].rearrange("p (k t) -> p k t", k=KC)[:, :, S * s:S * (s + 1)]
                nc.vector.tensor_tensor(cols, cols, own, ALU.add).then_inc(l1_added, 1)

            def layer2(c):
                dve.wait_ge(l2_low_done, 2 * c + 1)
                nc.vector.tensor_tensor(seqs(low[:, chunk(c)]), seqs(ps[:, 4]),
                                        per_seq(mask2[:, 16 * c:16 * c + 16]), ALU.mult)
                dve.wait_ge(l2_low_done, 2 * c + 2)
                nc.vector.tensor_tensor(seqs(low4[:, chunk(c)]), seqs(ps[0:R2, 5]),
                                        per_seq(mask24[0:R2, 16 * c:16 * c + 16]),
                                        ALU.mult).then_inc(l2_low4_masked, 1)
                dve.wait_ge(l2_low4_masked, c + 1)
                nc.vector.tensor_tensor(low[0:R2, chunk(c)], low[0:R2, chunk(c)], low4[:, chunk(c)],
                                        ALU.add).then_inc(l2_low_masked, 1)
                dve.wait_ge(l2_done, c + 1)
                for oc in range(KC):
                    add_to_x(oc, oc, c, l2_added)
                if c:
                    for kc in range(KC):
                        dve.wait_ge(l2_added, KC * c + kc + 1)
                        nc.vector.tensor_copy(x_hi[:, kc, chunk(c)], x_t[:, kc, chunk(c)]
                                              ).then_inc(x_hi_ready, 1)
                for kc in range(KC):
                    dve.wait_ge(x_hi_ready, KC * c + kc + 1)
                    nc.vector.tensor_tensor(x_lo[:, kc, chunk(c)], x_t[:, kc, chunk(c)],
                                            x_hi[:, kc, chunk(c)].bitcast(F32),
                                            ALU.subtract).then_inc(x_lo_ready, 1)

            def rope_tables():
                dve.wait_ge(sin_ready, 1)
                link(nc.vector.tensor_tensor(cos_t[:], sin_h[:], sin_h[:], ALU.mult))
                link(nc.vector.tensor_scalar(cos_t[:], cos_t[:], -2.0, 1.0, ALU.mult, ALU.add))
                half = HD // 2
                for n in range(2):
                    for h in range(2):
                        cols = slice(half * h, half * (h + 1))
                        w = norm_w[:, n, cols].unsqueeze(1).to_broadcast([P, TT, half])
                        nc.vector.tensor_tensor(rope_c[:, n, :, cols], cos_t[:], w, ALU.mult)
                        nc.vector.scalar_tensor_tensor(rope_s[:, n, :, cols], sin_t[:], 1.0 - 2.0 * h, w,
                                                       ALU.mult, ALU.mult)

            for c in range(TC):
                with dve.Fori(0, 2) as i:
                    for par in range(2):
                        dve.wait_ge(l1_done, 8 * i + (16 * c + 4 * par + 4))
                        for s in range(4):
                            add_l1(8 * i + (16 * c + 4 * par + s), s, par)
                if c == 0:
                    rope_tables()
                layer2(c)

            def heads(ap):
                return ap.rearrange("p (h d) -> p h d", h=4)

            def scale_tile(g, m, t, first):
                dve.wait_ge(summed, QKT * g + m + 1)
                dve.wait_ge(rstd_done, QKT * g + m + 1)
                if not (first and t < 2):
                    dve.wait_ge(qk_turned, QKT * g + m - 1)
                p = t % 2
                nc.vector.tensor_tensor(
                    heads(r_out[:, p]), heads(r_cos[:, p]),
                    stat[:, p, RSTD].unsqueeze(2).to_broadcast([P, 4, HD]), ALU.mult).then_inc(rn_done, 1)

            def newton_step(g, m, t):
                dve.wait_ge(y0_done, QKT * g + m + 1)
                y, v = stat[:, t % 2, Y0], stat[:, t % 2, VAR]
                w, r = stat[:, t % 2, NT], stat[:, t % 2, RSTD]
                nc.vector.tensor_tensor(w, y, y, ALU.mult).then_inc(newton, 1)
                dve.wait_ge(newton, 3 * (QKT * g + m) + 1)
                nc.vector.tensor_tensor(w, w, v, ALU.mult).then_inc(newton, 1)
                dve.wait_ge(newton, 3 * (QKT * g + m) + 2)
                nc.vector.tensor_scalar(w, w, -0.5, 1.5, ALU.mult, ALU.add).then_inc(newton, 1)
                dve.wait_ge(newton, 3 * (QKT * g + m) + 3)
                nc.vector.tensor_tensor(r, y, w, ALU.mult).then_inc(rstd_done, 1)

            def qk_tile(g, j, t, first, n):
                m = 8 * j + t
                p = t % 2
                dve.wait_ge(sq_done, QKT * g + m + 1)
                nc.vector.tensor_scalar(stat[:, p, VAR], stat[:, p, SQ], 1.0 / HD, EPS,
                                        ALU.mult, ALU.add).then_inc(var_done, 1)
                dve.wait_ge(var_done, QKT * g + m + 1)
                nc.vector.reciprocal(stat[:, p, INV], stat[:, p, VAR]).then_inc(inv_done, 1)
                if not (first and t < 2):
                    dve.wait_ge(rn_done, QKT * g + m - 1)
                for dst, tab in ((r_cos, rope_c), (r_sin, rope_s)):
                    ins = nc.vector.tensor_tensor(heads(dst[:, p]), heads(ps[:, t % 4]),
                                                  tab[:, n, t].unsqueeze(1).to_broadcast([P, 4, HD]), ALU.mult)
                ins.then_inc(roped, 1)
                if not (first and t == 0):
                    scale_tile(g, m - 1, (t - 1) % 8, first and t - 1 < 2)
                newton_step(g, m, t)

            def split_k(g, i, e):
                b2, k = e // 4, e % 4
                dve.wait_ge(k_hi_done, UNITS * g + 8 * i + (e + 1))
                nc.vector.tensor_tensor(k_lo[:, :, k], k_buf[b2][:, :, k], k_hi[:, :, k].bitcast(F32),
                                        ALU.subtract).then_inc(k_lo_done, 1)

            def split_q(g, b, b2, half):
                n = QH // 2
                dve.wait_ge(q_hi_done, 2 * B * g + 2 * b + (half + 1))
                nc.vector.tensor_tensor(
                    q_lo[b2][:, n * half:n * (half + 1)],
                    qk[:, ds(b, 1), KVH + n * half:KVH + n * (half + 1), :].rearrange("p b h t -> p (b h) t"),
                    q_hi[b2][:, n * half:n * (half + 1)].bitcast(F32), ALU.subtract)

            def normalise(g, s, c):
                p = c % 2
                dve.wait_ge(inv_l, UNITS * g + s + 1)
                dve.wait_ge(pv_done, UNITS * g + s + 1)
                if c >= 2:
                    dve.wait_ge(o_turned, UNITS * g + s - 1)
                nc.vector.tensor_scalar(o_sb[:, p], ps[:, 6, 0:P], row_inv[:, p:p + 1], None,
                                        ALU.mult).then_inc(o_norm, 1)

            def batch_mask(g, b, p, first):
                if not first:
                    dve.wait_ge(max_done, UNITS * g + 4 * b - 4)
                nc.vector.tensor_scalar(mask[:, p, 0:L], iota16[:], len_b[:, ds(b, 1)], NEG,
                                        ALU.is_ge, ALU.mult).then_inc(mask_done, 1)

            def unit_step(g, i, e, c):
                s = 8 * i + e
                p = c % 2
                if 2 <= c < UNITS + 2:
                    dve.wait_ge(exp_done, UNITS * g + s - 1)
                    if c >= 4:
                        dve.wait_ge(o_norm, UNITS * g + s - 3)
                    nc.vector.reciprocal(row_inv[:, p:p + 1], row_sum[:, p:p + 1]).then_inc(inv_l, 1)
                if c < UNITS:
                    b = 2 * i + e // 4
                    nxt = i + (e + 1) // 8, (e + 1) % 8
                    if c < UNITS - 1 and nxt[1] % 4:
                        split_k(g, *nxt)
                    if e % 4 == 0:
                        dve.wait_ge(mask_done, (B + 1) * g + b + 1)
                    dve.wait_ge(s_done, UNITS * g + s + 1)
                    settle(dve)
                    nc.vector.tensor_tensor_reduce(
                        out=sm[:, p], in0=ps[:, 2 * p:2 * p + 2].rearrange("p b n -> p (b n)")[:, SC:SC + KEYS],
                        in1=mask[:, e // 4], scale=-SCALE, scalar=BIG, op0=ALU.add, op1=ALU.min,
                        accum_out=sm_min[:, p:p + 1]).then_inc(max_done, 1)
                    if c < UNITS - 1 and nxt[1] % 4 == 0:
                        split_k(g, *nxt)
                    if e % 4 == 0:
                        batch_mask(g, b + 1, 1 - e // 4, c < 4)
                if 1 <= c <= UNITS:
                    dve.wait_ge(p_turned, UNITS * g + s)
                    if c >= 3:
                        dve.wait_ge(pv_done, UNITS * g + s - 2)
                    nc.vector.tensor_copy(pt[:, 1 - p, 0:PTA * P], ps[:, 4, 0:PTA * P]).then_inc(pt_a, 1)
                if 2 <= c < UNITS + 2:
                    normalise(g, s - 2, c - 2)
                if c < UNITS - 4 and e % 4 in (1, 2):
                    split_q(g, 2 * i + (e // 4 + 1), 1 - e // 4, e % 4 - 1)

            with dve.Fori(0, HALVES) as g:
                for t in range(TT):
                    qk_tile(g, 0, t, True, 0)
                with dve.Fori(0, 2) as i:
                    for e in range(2):
                        for t in range(TT):
                            qk_tile(g, 2 * i + (1 + e), t, False, 1)
                scale_tile(g, QKT - 1, 7, False)
                dve.wait_ge(proj_done, PROJ * g + PROJ)
                settle(dve)
                split_q(g, 0, 0, 0)
                split_k(g, 0, 0)
                nc.vector.memset(mask[:, :, L:KEYS], 0.0)
                batch_mask(g, 0, 0, True)
                nc.vector.memset(pr[:, :, KEYS:KPAD], 0.0)
                split_q(g, 0, 0, 1)
                for c in range(8):
                    unit_step(g, 0, c, c)
                with dve.Fori(1, UNITS // 8 - 1) as i:
                    for e in range(8):
                        unit_step(g, i, e, 8 + e)
                for e in range(8):
                    unit_step(g, UNITS // 8 - 1, e, UNITS - 8 + e)
                for e in range(2):
                    unit_step(g, UNITS // 8, e, UNITS + e)
                dve.wait_ge(pv_done, UNITS * (g + 1))
                for q in range(OBLK):
                    for c in range(TC):
                        for pair in range(2):
                            dve.wait_ge(o_hi_ready, 16 * g + 4 * q + 2 * c + pair + 1)
                            nc.vector.tensor_tensor(
                                o_lo[:, pair].rearrange("p h (b t) -> p b h t", t=S),
                                qk[:, 16 * c:16 * (c + 1), KVH + 4 * q + 2 * pair:KVH + 4 * q + 2 * pair + 2, :],
                                o_hi[:, pair].bitcast(F32).rearrange("p h (b t) -> p b h t", t=S),
                                ALU.subtract).then_inc(o_lo_ready, 1)
                    if q == 1:
                        for c in range(TC):
                            for kc in range(KC):
                                dve.wait_ge(x_hi_ready, TC * KC * (g + 1) + KC * c + kc + 1)
                                nc.vector.tensor_tensor(
                                    x_lo[:, kc, chunk(c)], x_t[:, kc, chunk(c)],
                                    x_hi[:, kc, chunk(c)].bitcast(F32), ALU.subtract).then_inc(x_lo_ready, 1)
                for c in range(TC):
                    dve.wait_ge(d_done, 16 * g + 14 + 2 * c + D_AHEAD)
                    for oc in range(KC):
                        add_to_x(KC * c + oc, oc, c, d_added)

        @block.tensor
        def _(pe):
            def mm(o, lhsT, rhs, start, stop):
                return nc.tensor.matmul(o, lhsT, rhs, start=start, stop=stop)

            pe.wait_ge(w0b_in, 16)
            for c in range(TC):
                for kc in range(KC):
                    if c == 0 and kc % 2 == 0:
                        pe.wait_ge(x_in[kc // 2], 16)
                    elif kc == 0:
                        pe.wait_ge(x_in[2], 16)
                    ins = mm(ps[:, c], w0b[:, kc], x_t[:, kc, chunk(c)], kc == 0, kc == KC - 1)
                ins.then_inc(l0_low_done, 1)
            pe.wait_ge(w0a_in, 16)
            for c in range(TC):
                pe.wait_ge(l0_low_masked, TC if c else 1)
                for oc in range(KC):
                    mm(ps[:, (2 + KC * c + oc) % 8], w0a[:, tile(oc)], low[:, chunk(c)], True,
                       True).then_inc(l0_done, 1)

            def expert(t, s, par):
                b = 4 * t + s
                pe.wait_ge(exp_in[s], 16 * t + 16)
                pe.wait_ge(l1_added, b + 1)
                for oc in range(KC):
                    for kc in range(KC):
                        ins = mm(ps[:, 4 - 4 * par + s, tile(oc)], w_exp[:, s, kc, tile(oc)],
                                 x_t[:, kc, ds(P * t, P)], kc == 0, kc == KC - 1)
                ins.then_inc(l1_done, 1)

            pe.wait_ge(l0_added, TC * KC)
            for c in range(TC):
                if c:
                    pe.wait_ge(l2_low_masked, c)
                with pe.Fori(0, 2) as i:
                    for par in range(2):
                        if c and par:
                            pe.wait_ge(l2_added, KC * c)
                        for s in range(4):
                            expert(2 * i + (4 * c + par), s, par)
                pe.wait_ge(l1_added, 16 * (c + 1) + L1_AHEAD)
                if c == 0:
                    pe.wait_ge(w2_in, 16 * 6)
                    pe.wait_ge(l0_added, TC * KC)
                else:
                    pe.wait_ge(l2_added, KC)
                for n, (cols, o) in enumerate(((slice(0, P), ps[:, 4]), (slice(P, N2 * R2), ps[0:R2, 5]))):
                    for kc in range(KC):
                        ins = mm(o, w2a[:, kc, cols], x_t[:, kc, chunk(c)], kc == 0, kc == KC - 1)
                    ins.then_inc(l2_low_done, 1)
                for oc in range(KC):
                    for kc in range(KC):
                        mm(ps[:, oc], w2[:, kc, tile(oc)], x_t[:, kc, chunk(c)], kc == 0, False)
                pe.wait_ge(l2_low_masked, c + 1)
                for oc in range(KC):
                    ins = mm(ps[:, oc], w2b[:, tile(oc)], low[:, chunk(c)], False, True)
                ins.then_inc(l2_done, 1)

            def project(t, par, n_w=None):
                for kc in range(KC):
                    if n_w is not None:
                        pe.wait_ge(w_lo_done, n_w + LO_AHEAD + PIECES // KC * (kc + 1))
                    for n, (x, w) in enumerate(((x_hi, w_hi), (x_hi, w_lo), (x_lo, w_hi))):
                        ins = mm(ps[:, t % 4], x[:, kc, tile(t)], w[par][:, chunk(kc)],
                                 kc == 0 and n == 0, kc == KC - 1 and n == 2)
                ins.then_inc(proj_done, 1)

            def turn_qk(g, m, t, first):
                pe.wait_ge(rn_done, QKT * g + m + 1)
                if not (first and t < 2):
                    pe.wait_ge(qk_stored, QKT * g + m - 1)
                for h in range(4):
                    ins = nc.tensor.transpose(ps[:, 4 + t % 2, tile(h)], r_out[:, t % 2, tile(h)], ident)
                ins.then_inc(qk_turned, 1)

            def block_of(g, j, par, first):
                if not first:
                    pe.wait_ge(w_lo_done, PIECES * (NBLK * g + j + 1) + LO_AHEAD)
                for t in range(TT):
                    m = 8 * j + t
                    if first and t % 4 == 0:
                        pe.wait_ge(x_lo_ready, TC * KC * g + KC * (t // 4 + 1))
                    if first and t < 4:
                        pe.wait_ge(l2_added, KC + t + 1)
                        pe.wait_ge(d_added, 8 * g + ADD_AHEAD - 7 + t)
                    else:
                        pe.wait_ge(roped, QKT * g + m - 3)
                    project(t, par, PIECES * NBLK * g if first and t == 0 else None)
                    if t >= TLAG:
                        turn_qk(g, m - TLAG, t - TLAG, first)
                    elif not first:
                        turn_qk(g, m - TLAG, t - TLAG + TT, False)

            def scores(g, s, c, e):
                p, b2, k = c % 2, e // 4, e % 4
                pe.wait_ge(k_lo_done, UNITS * g + s + 1)
                if c < 2:
                    pe.wait_ge(v_copied, 8 * g + TT - 2 + 2 * c)
                else:
                    pe.wait_ge(max_done, UNITS * g + s - 1)
                for o, pages in ((ps[:, 2 * p, SC:512], slice(0, KA)),
                                 (ps[:, 2 * p + 1, 0:KEYS - KA * S], slice(KA, NPP + 1))):
                    for n, (q, kt) in enumerate(((q_hi, k_hi), (q_hi, k_lo), (q_lo, k_hi))):
                        ins = mm(o, q[b2][:, REP * k:REP * (k + 1), :].rearrange("p h t -> p (h t)"),
                                 kt[:, pages, k], n == 0, n == 2)
                ins.then_inc(s_done, 1)

            def values(g, s, c, e):
                p, b2, k = c % 2, e // 4, e % 4
                pe.wait_ge(pt_a, UNITS * g + s + 1)
                pe.wait_ge(pt_b, UNITS * g + s + 1)
                if k == 0:
                    pe.wait_ge(v_in[b2], 16 * VCH * nth_v[0] + 16 * VCH)
                    pe.wait_ge(vn_in[b2], 16 * nth_v[0] + 16)
                if c >= 1:
                    pe.wait_ge(o_norm, UNITS * g + s)
                for ch in range(KCH):
                    ins = mm(ps[:, 6, 0:P], pt[:, p, tile(ch)], v_buf[b2][:, ch, HD * k:HD * (k + 1)],
                             ch == 0, ch == KCH - 1)
                ins.then_inc(pv_done, 1)

            def turn_o(g, s, c, e, b):
                pe.wait_ge(o_norm, UNITS * g + s + 1)
                if e % 4 == 0 and c >= 4:
                    pe.wait_ge(o_stored, B * g + b)
                nc.tensor.transpose(ps[:, 7, tile(e % 4)], o_sb[:, c % 2], ident).then_inc(o_turned, 1)

            def turn_p(g, s, c):
                pe.wait_ge(exp_done, UNITS * g + s + 1)
                if c >= 1:
                    pe.wait_ge(pt_a, UNITS * g + s)
                    pe.wait_ge(pt_b, UNITS * g + s)
                for ch in range(KCH):
                    o = ps[:, 4, tile(ch)] if ch < PTA else ps[:, 5, tile(ch - PTA)]
                    ins = nc.tensor.transpose(o, pr[:, c % 2, tile(ch)], ident)
                ins.then_inc(p_turned, 1)

            nth_v = [0]

            def unit_step(g, i, e, c):
                s = 8 * i + e
                nth_v[0] = 16 * g + i + (0 if e >= 2 else -1)
                if c < UNITS:
                    scores(g, s, c, e)
                if 1 <= c <= UNITS:
                    turn_p(g, s - 1, c - 1)
                if 2 <= c < UNITS + 2:
                    values(g, s - 2, c - 2, (e - 2) % 8)
                if 3 <= c:
                    turn_o(g, s - 3, c - 3, (e - 3) % 8, 2 * i + (e - 3) // 4)

            with pe.Fori(0, HALVES) as g:
                block_of(g, 0, 0, True)
                with pe.Fori(0, 2) as i:
                    for e in range(2):
                        block_of(g, 2 * i + (1 + e), 1 - e, False)
                pe.wait_ge(w_lo_done, PIECES * (NBLK * g + BLK) + LO_AHEAD)
                for t in range(TT):
                    if t < 4:
                        pe.wait_ge(roped, QKT * g + QKT + t - 3)
                    else:
                        pe.wait_ge(v_copied, 8 * g + t - 3)
                    project(t, 1)
                    if t < TLAG:
                        turn_qk(g, QKT - TLAG + t, TT - TLAG + t, False)
                for c in range(8):
                    unit_step(g, 0, c, c)
                with pe.Fori(1, UNITS // 8) as i:
                    for e in range(8):
                        unit_step(g, i, e, 8 + e)
                for e in range(3):
                    unit_step(g, UNITS // 8, e, UNITS + e)
                for q in range(OBLK):
                    par = q % 2
                    pe.wait_ge(w_lo_done, PIECES * (NBLK * g + BLK + q + 1) + LO_AHEAD)
                    for c in range(TC):
                        for pair in range(2):
                            pe.wait_ge(o_lo_ready, 16 * g + 4 * q + 2 * c + pair + 1)
                            for h in range(2):
                                for oc in range(KC):
                                    cols = slice(512 * (2 * pair + h) + P * oc, 512 * (2 * pair + h) + P * (oc + 1))
                                    for n, (w, o) in enumerate(((w_hi, o_hi), (w_hi, o_lo), (w_lo, o_hi))):
                                        ins = mm(ps[:, KC * c + oc], w[par][:, cols], o[:, pair, h],
                                                 q == 0 and pair == 0 and h == 0 and n == 0,
                                                 q == OBLK - 1 and pair == 1 and h == 1 and n == 2)
                            ins.then_inc(d_done, 1)


def kernel(x, itok_B_3_7, itok_B_0_15, itok_B_0_2, itok_Bx16_0_63, itok_B_207_1644,
           L0_cond_A, L0_cond_B, L1_cond_weight, L2_cond_W, L2_cond_lora_A, L2_cond_lora_B_w,
           L3_cond_Wq, L3_cond_Wk, L3_cond_Wv, L3_cond_Wo, L3_cond_q_norm_w, L3_cond_k_norm_w,
           L3_cond_k_cache, L3_cond_v_cache):
    import numpy as np
    import concourse.bacc as bacc
    from concourse.bass_utils import run_bass_kernel_spmd

    def fold(w):
        w = np.asarray(w)
        return w.reshape(w.shape[0], KC, P).transpose(2, 1, 0)

    def blocks(w, g, n):
        w = np.asarray(w)[g * n * 512:(g + 1) * n * 512]
        return [fold(w[512 * j:512 * (j + 1)]).reshape(P, BW) for j in range(n)]

    wo = np.asarray(L3_cond_Wo).reshape(DM, HALVES, OBLK, 4, HD).transpose(1, 2, 4, 3, 0)
    l3_w = []
    for g in range(HALVES):
        l3_w += blocks(L3_cond_Wk, g, 1) + blocks(L3_cond_Wq, g, OBLK) + blocks(L3_cond_Wv, g, 1)
        l3_w += [wo[g, j].reshape(P, BW) for j in range(OBLK)]
    kc = np.asarray(L3_cond_k_cache).reshape(PAGES, PSIZE, HALVES, KVH, HD).transpose(2, 0, 4, 3, 1)
    kc = np.ascontiguousarray(kc)
    vc = np.asarray(L3_cond_v_cache).reshape(PAGES, PSIZE, HALVES, KVH * HD).transpose(2, 0, 1, 3)
    const = np.zeros((P, C_N), np.float32)
    rows = np.arange(P)
    const[:, C_ID:C_ID + P] = np.eye(P)
    const[:, C_P16], const[:, C_P32], const[:, C_M32], const[:, C_P] = rows // R0, rows // R2, rows % S, rows
    const[:, C_FREQ:] = 1.0 / 10000.0 ** (np.arange(0, HD, 2) / HD)
    lora_a = np.asarray(L2_cond_lora_A)
    lens, pages = np.asarray(itok_B_207_1644), np.asarray(itok_Bx16_0_63)
    arrays = {
        "lens_q": lens.reshape(TT, BPT).T, "pages_q": pages.reshape(B, VCH, P // PSIZE).transpose(2, 0, 1),
        "pages_k": pages[:, SPP:],
        "x_t": fold(np.asarray(x).reshape(T, DM)),
        "ids0": itok_B_3_7, "ids1": itok_B_0_15, "ids2": itok_B_0_2,
        "pages": pages, "lens": lens,
        "l0_b": fold(np.asarray(L0_cond_B).reshape(N0 * R0, DM)),
        "l0_a": np.asarray(L0_cond_A).transpose(0, 2, 1).reshape(N0 * R0, DM),
        "l1_w": np.asarray(L1_cond_weight).reshape(16, DM, KC, P).transpose(0, 3, 2, 1),
        "l2_w": fold(L2_cond_W),
        "l2_a": fold(lora_a.transpose(0, 2, 1).reshape(N2 * R2, DM)),
        "l2_b": np.asarray(L2_cond_lora_B_w).T,
        "l3_w": np.stack(l3_w),
        "k_norm": L3_cond_k_norm_w, "q_norm": L3_cond_q_norm_w,
        "k_t": kc.reshape(HALVES * PAGES, HD, KVH, PSIZE),
        "k_rows": kc.reshape(HALVES * PAGES * HD, KVH * PSIZE),
        "v_rows": vc.reshape(HALVES * PAGES * PSIZE, KVH * HD),
        "consts": const, "iota": np.arange(L, dtype=np.float32),
    }
    arrays = {f"in_{n}": np.ascontiguousarray(v) for n, v in arrays.items()}
    nc = bacc.Bacc("TRN2", target_bir_lowering=False, num_devices=1)
    a = {n[3:]: nc.dram_tensor(n, v.shape, mybir.dt.from_np(v.dtype), kind="ExternalInput").ap()
         for n, v in arrays.items()}
    a["v_new"] = nc.dram_tensor("v_new_dram", [HALVES * B, S, KVH * HD], F32, kind="Internal").ap()
    out = nc.dram_tensor("out_t", [P, KC, T], F32, kind="ExternalOutput").ap()
    build(nc, a, out)
    r = run_bass_kernel_spmd(nc, [arrays], core_ids=[0])
    got = np.asarray(r.results[0]["out_t"])
    return np.ascontiguousarray(got.transpose(2, 1, 0).reshape(B, S, DM))
```
